# Optimizing a Trainium2 kernel written in Bass

```python
import numpy as np
import jax
import jax.numpy as jnp

def _softmax(x, axis=-1):
    return jax.nn.softmax(x, axis=axis)

def _gelu(x):
    return jax.nn.gelu(x, approximate=True)

def _silu(x):
    return jax.nn.silu(x)

def _sigmoid(x):
    return jax.nn.sigmoid(x)

def _layernorm(x, axis=-1, eps=1e-05):
    m = jnp.mean(x, axis=axis, keepdims=True)
    v = jnp.var(x, axis=axis, keepdims=True)
    return (x - m) / jnp.sqrt(v + eps)

def _scatter_add(tgt, idx, src, axis=0):
    return tgt.at[idx].add(src)

def _segment_sum(src, seg, n):
    return jax.ops.segment_sum(src, seg, n)
kernel_name = 'mk_xattn_ffn_d1_seqx_r4_1576ee'

def setup_inputs(seed: int=0):
    np.random.seed(seed)
    _w = jnp.asarray

    def _rec_inputs():
        import jax
        import jax.numpy as jnp
        _rk = jax.random.key(seed)
        x = 7.22e-05 + 1 * jax.random.normal(jax.random.fold_in(_rk, 1), (32, 128, 512), jnp.float32)
        _lenS = 128 - jax.random.randint(jax.random.fold_in(_rk, 7), (32,), 0, max(1, 128 // 4) + 1, jnp.int32)
        _lenS2 = 128 - jax.random.randint(jax.random.fold_in(_rk, 8), (32,), 0, max(1, 128 // 4) + 1, jnp.int32)
        _ctx_2048P = jax.random.normal(jax.random.fold_in(_rk, 11), (32, 16, 512), jnp.float32)
        _ctx_2048c = jax.random.dirichlet(jax.random.fold_in(_rk, 511), 0.3 * jnp.ones((16,), jnp.float32), (32, 128))
        _ctx_2048t = jnp.einsum('bsk,bkd->bsd', _ctx_2048c, _ctx_2048P)
        _ctx_2048t = _ctx_2048t * jax.lax.rsqrt(jnp.mean(jnp.square(_ctx_2048t)) + 1e-12) * 0.953939
        ctx_2048 = 4.13588e-05 + 0.999923 * (_ctx_2048t + 0.3 * jax.random.normal(jax.random.fold_in(_rk, 611), (32, 128, 512), jnp.float32))
        return (x, ctx_2048)
    x, ctx_2048 = _rec_inputs()

    def _L0_xattn_setup():
        import jax, jax.numpy as jnp
        import numpy as np
        N_HEAD = 8
        key = jax.random.key(seed)
        k1, k2, k3 = jax.random.split(key, 3)
        b, d, m = (4, 256, 512)
        c, n = (256, 512)
        q = jax.random.normal(k1, (b, d, m), dtype=jnp.float32)
        k = jax.random.normal(k2, (d // d * b, d, n), dtype=jnp.float32).reshape(b, d, n)
        v = jax.random.normal(k3, (b, c, n), dtype=jnp.float32)
        return {'q': q, 'k': k, 'v': v}
    _L0_xattn_all = _L0_xattn_setup()
    _L0_xattn_in = {k: v for k, v in _L0_xattn_all.items() if k in ()}
    del _L0_xattn_all

    def _L0_ffn_setup():
        import jax, jax.numpy as jnp
        import numpy as np
        DIM = 512
        HIDDEN = 2048
        NUM_EXPERTS = 2
        BATCH, SEQ = (4, 256)
        key = jax.random.key(seed)
        k1, k2, k3, k4 = jax.random.split(key, 4)
        x = jax.random.normal(k1, (BATCH, SEQ, DIM), dtype=jnp.float32)
        w_router = jax.random.normal(k2, (NUM_EXPERTS, DIM), dtype=jnp.float32) * (1.0 / np.sqrt(DIM))
        w_fc = jax.random.normal(k3, (NUM_EXPERTS, HIDDEN, DIM), dtype=jnp.float32) * (1.0 / np.sqrt(DIM))
        w_proj = jax.random.normal(k4, (NUM_EXPERTS, DIM, HIDDEN), dtype=jnp.float32) * (1.0 / np.sqrt(HIDDEN))
        return {'x': x, 'w_router': w_router, 'w_fc': w_fc, 'w_proj': w_proj}
    _L0_ffn_all = _L0_ffn_setup()
    _L0_ffn_in = {k: v for k, v in _L0_ffn_all.items() if k in ('w_router', 'w_fc', 'w_proj')}
    del _L0_ffn_all
    return {'x': x, 'ctx_2048': ctx_2048, 'L0_ffn_w_router': _L0_ffn_in['w_router'], 'L0_ffn_w_fc': _L0_ffn_in['w_fc'], 'L0_ffn_w_proj': _L0_ffn_in['w_proj']}

def reference(x, ctx_2048, L0_ffn_w_router, L0_ffn_w_fc, L0_ffn_w_proj):
    import jax
    import jax.numpy as jnp

    def _L0_xattn_ref(q, k, v):
        import jax, jax.numpy as jnp
        import numpy as np
        N_HEAD = 8
        b, d, m = q.shape
        c = v.shape[1]
        h = N_HEAD
        qh = q.reshape(b * h, d // h, m)
        kh = k.reshape(b * h, d // h, -1)
        vh = v.reshape(b * h, c // h, -1)
        scale = 1.0 / jnp.sqrt(jnp.asarray(d // h, dtype=q.dtype))
        qk = jnp.einsum('bdm,bdn->bmn', qh, kh) * scale
        sm = jax.nn.softmax(qk, axis=-1)
        ret = jnp.einsum('bmn,bcn->bcm', sm, vh)
        return ret.reshape(b, c, m)

    def _L0_ffn_ref(x, w_router, w_fc, w_proj):
        import jax, jax.numpy as jnp
        import numpy as np
        DIM = 512
        HIDDEN = 2048
        NUM_EXPERTS = 2
        BATCH, SEQ = (4, 256)
        bsz, seq, dim = x.shape
        num_experts = w_router.shape[0]
        x_flat = x.reshape(-1, dim)
        logits = x_flat @ w_router.T
        probs = jax.nn.softmax(logits, axis=-1)
        top_idx = jnp.argmax(probs, axis=-1)
        top_weight = jnp.take_along_axis(probs, top_idx[:, None], axis=1)[:, 0]
        h = jnp.einsum('nd,ehd->enh', x_flat, w_fc)
        a = jnp.square(jnp.where(h >= 0, h, 0.5 * h))
        expert_out = jnp.einsum('enh,edh->end', a, w_proj)
        mask = (top_idx[None, :] == jnp.arange(num_experts)[:, None]).astype(x.dtype)
        out = jnp.einsum('end,en->nd', expert_out, mask * top_weight[None, :])
        return out.reshape(bsz, seq, dim)
    x = x + _L0_xattn_ref(_layernorm(x, axis=-1), ctx_2048, ctx_2048)
    x = x + _L0_ffn_ref(_layernorm(x, axis=-1), L0_ffn_w_router, L0_ffn_w_fc, L0_ffn_w_proj)
    return x

_drawn_inputs = setup_inputs


def setup_inputs(seed=0):
    import zlib

    import numpy as np

    out = dict(_drawn_inputs(seed))
    spreads = {}
    factors = {}
    for name, (base, spread) in spreads.items():
        noise = np.random.default_rng([zlib.crc32(name.encode()), seed]).standard_normal(out[name].shape)
        drawn = base * np.exp(spread * noise) if base else spread * noise
        out[name] = jnp.asarray(drawn.astype(out[name].dtype))
    for name, factor in factors.items():
        out[name] = (out[name] * factor).astype(out[name].dtype)
    return out
```

```python
from contextlib import ExitStack

import concourse.bass as bass
from concourse import mybir

ALU = mybir.AluOpType
ACT = mybir.ActivationFunctionType
AX = mybir.AxisListType
F32 = mybir.dt.float32
BF16 = mybir.dt.bfloat16
I32 = mybir.dt.int32

P = 128


def wait(eng, sem, value):
    if not isinstance(value, int) or value > 0:
        eng.wait_ge(sem, value)


def build_program(nc, x, ctx, w_router, w_fc, w_proj, out):
    NB, D, M = x.shape
    H = 8
    DH = D // H
    NCH = M // P
    GH = 4
    NG = H // GH
    NQ = NG * NCH
    NE, HID, _ = w_fc.shape
    NTOK = NB * D
    CAP = NTOK + P
    NT = CAP // P
    KC = M // P
    HS = HID // 512
    ROW = M + 4
    LEAD = 4
    SPLIT = 6
    KR = SPLIT * DH
    EPS = 1e-5
    SCALE = 1.0 / float(DH) ** 0.5
    RING = 3
    K_PART = [0, 1, 0, 1, 2, 0]
    Q_PART = [0, 0, 1, 1, 0, 2]
    assert D == P and M == 512 and NQ == H and NB == NE * HID // P

    sorted_rows = nc.dram_tensor("sorted_rows", (CAP, ROW), F32, kind="Internal").ap()
    wproj_t = nc.dram_tensor("wproj_t", (P, NE, HID // P, M), F32, kind="Internal").ap()
    x_dh = x.rearrange("b (h d) m -> b d h m", d=DH)
    ctx_dh = ctx.rearrange("b (h d) m -> b d h m", d=DH)
    wfc_rows = w_fc.rearrange("e (r p) d -> (e r) p d", p=P)
    wpr_rows = w_proj.rearrange("e (r p) n -> (e r) p n", p=P)

    def wfc_block(n):
        return wfc_rows[n]

    def wpr_block(n):
        return wpr_rows[n // 4, :, bass.ds((n % 4) * 512, 512)]

    with ExitStack() as outer:
        def sem(name):
            return outer.enter_context(nc.semaphore(name))

        def psum(name, shape):
            return outer.enter_context(nc.psum_tensor(name, shape, F32))

        def keep(name, shape, dt):
            return outer.enter_context(nc.sbuf_tensor(name, shape, dt))

        s_pair = [psum("s_pair0", [P, 2, 512]), psum("s_pair1", [P, 2, 512])]
        st_bank = [psum("st_bank0", [P, 512]), psum("st_bank1", [P, 512])]
        o_bank, m_bank = psum("o_bank", [P, 512]), psum("m_bank", [P, 512])

        ident = keep("ident", [P, P], F32)
        left_mark = keep("left_mark", [P, 1], F32)
        left_mark2 = keep("left_mark2", [P, 1], F32)
        neghalf = keep("neghalf", [P, 1], F32)
        expert_of = keep("expert_of", [1, NT], I32)
        wfc_sb = keep("wfc_sb", [P, NE, KC, HID], F32)

        inner = ExitStack()

        def sb(name, shape, dt):
            return inner.enter_context(nc.sbuf_tensor(name, shape, dt))

        kst = sb("kst", [P, RING, H, M], BF16)
        qst = sb("qst", [P, RING, H, M], BF16)
        probs = sb("probs", [P, 4, GH, M], F32)
        x_in = sb("x_in", [P, M], F32)
        c_in = sb("c_in", [P, M], F32)
        x_res = sb("x_res", [P, M], F32)
        kparts = sb("kparts", [P, 3, M], BF16)
        qparts = sb("qparts", [P, 3, M], BF16)
        krest = sb("krest", [P, M], F32)
        qrest = sb("qrest", [P, M], F32)
        qf = sb("qf", [P, M], F32)
        vt = sb("vt", [P, H, NCH, 2 * DH], F32)
        vt_next = sb("vt_next", [P, RING, H, NCH, DH], F32)
        max_head = sb("max_head", [P, LEAD * NCH], F32)
        maxes = sb("maxes", [P, H * NCH], F32)
        cparts = sb("cparts", [H * NCH, 2, P], BF16)
        crest = sb("crest", [H * NCH, P], F32)
        o_sb = sb("o_sb", [P, NG, M], F32)
        o_norm = sb("o_norm", [P, NCH, D], F32)
        rsum = sb("rsum", [P, NCH, GH], F32)
        row = sb("row", [P, ROW], F32)
        xln = sb("xln", [P, M], F32)
        prod = sb("prod", [P, M], F32)
        wr = sb("wr", [P, NE, M], F32)
        wdiff = sb("wdiff", [P, M], F32)
        stats1 = sb("stats1", [P, 6], F32)
        mv1 = sb("mv1", [P, 2], F32)
        ve1 = sb("ve1", [P, 1], F32)
        rstd1 = sb("rstd1", [P, 1], F32)
        stats2 = sb("stats2", [P, 6], F32)
        ve2 = sb("ve2", [P, 1], F32)
        to_one = sb("to_one", [P, 1], BF16)
        upper = sb("upper", [P, P], BF16)
        ones = sb("ones", [P, P], BF16)
        count1 = sb("count1", [P, 1], F32)
        ident_i = sb("ident_i", [P, 1], I32)
        token = sb("token", [P, 1], F32)
        neg_a = sb("neg_a", [P, 1], F32)
        neg_b = sb("neg_b", [P, 1], F32)
        ranks = sb("ranks", [P, 2], F32)
        slot = sb("slot", [P, 1], I32)
        pad_row = sb("pad_row", [P, ROW], F32)
        pad_slot = sb("pad_slot", [P, 1], I32)
        pad_f = sb("pad_f", [P, 1], F32)
        starts_i = sb("starts_i", [1, NT], I32)
        starts = sb("starts", [1, NT], F32)
        wst = [sb("wst0", [P, 512], F32), sb("wst1", [P, 512], F32)]
        wpr_out = sb("wpr_out", [P, NCH, P], F32)
        inner.close()

        second = outer.enter_context(ExitStack())

        def sb2(name, shape, dt):
            return second.enter_context(nc.sbuf_tensor(name, shape, dt))

        wpr_sb = sb2("wpr_sb", [P, NE, HID // P, M], F32)
        rows_in = sb2("rows_in", [P, 2, ROW], F32)
        f_ln = sb2("f_ln", [P, M], F32)
        f_lnt = sb2("f_lnt", [P, KC, P], F32)
        half_h = sb2("half_h", [P, 2, 512], F32)
        leaky = sb2("leaky", [P, 2, 512], F32)
        act = sb2("act", [P, 2, 512], F32)
        act_t = sb2("act_t", [P, HID // P, P], F32)
        absd = sb2("absd", [P, 1], F32)
        negd = sb2("negd", [P, 1], F32)
        expd = sb2("expd", [P, 1], F32)
        den = sb2("den", [P, 1], F32)
        top_w = sb2("top_w", [P, 1], F32)
        y_out = sb2("y_out", [P, M], F32)
        y_token = sb2("y_token", [P, 1], I32)

        h_bank = [s_pair[0][:, 0, :], s_pair[1][:, 0, :]]
        at_bank, y_bank, xt_bank = st_bank, o_bank, m_bank

        x_loaded, c_loaded, res_loaded = sem("x_loaded"), sem("c_loaded"), sem("res_loaded")
        wr_loaded = sem("wr_loaded")
        wst_loaded = [sem("wst_loaded0"), sem("wst_loaded1")]
        const_a, const_ready = sem("const_a"), sem("const_ready")
        v_const = sem("v_const")
        wdiff_ready = sem("wdiff_ready")
        k1_done, krest_done, k2_done, k3_done = (sem(n) for n in ("k1_done", "krest_done", "k2_done", "k3_done"))
        q1_done, qrest_done, q2_done, q3_done = (sem(n) for n in ("q1_done", "qrest_done", "q2_done", "q3_done"))
        stats1_done, mv1_done, ve1_done, rstd1_done, q_done = (
            sem(n) for n in ("stats1_done", "mv1_done", "ve1_done", "rstd1_done", "q_done"))
        k_stacked, q_stacked = sem("k_stacked"), sem("q_stacked")
        scored, maxed, head_copied = sem("scored"), sem("maxed"), sem("head_copied")
        max_t, c1_done, crest_done, c2_done, c_stacked = (
            sem(n) for n in ("max_t", "c1_done", "crest_done", "c2_done", "c_stacked"))
        shifted, exped, pv_done = sem("shifted"), sem("exped"), sem("pv_done")
        v_t, v_half = sem("v_t"), [sem("v_half0"), sem("v_half1")]
        o_moved = [sem("o_moved0"), sem("o_moved1")]
        o_t = [sem("o_t0"), sem("o_t1")]
        rsum_done = [sem("rsum_done0"), sem("rsum_done1")]
        o_normed = [sem("o_normed0"), sem("o_normed1")]
        o_back, mid_done = sem("o_back"), sem("mid_done")
        stats2_done, mv2_done, ve2_done, rstd2_done = (
            sem(n) for n in ("stats2_done", "mv2_done", "ve2_done", "rstd2_done"))
        xln_done, ldiff_done, one_done, ranked, nega_done, negb_done = (
            sem(n) for n in ("xln_done", "ldiff_done", "one_done", "ranked", "nega_done", "negb_done"))
        slot_done, count_done, token_done, row_done, scattered = (
            sem(n) for n in ("slot_done", "count_done", "token_done", "row_done", "scattered"))
        guest_read = sem("guest_read")
        pad_a, pad_done, table_a, table_done, padded = (
            sem(n) for n in ("pad_a", "pad_done", "table_a", "table_done", "padded"))
        w_t = [sem("w_t0"), sem("w_t1")]
        wpr_stored = sem("wpr_stored")
        wpr_loaded, rows_loaded = sem("wpr_loaded"), sem("rows_loaded")
        f_ln_done, f_t, f_t_moved = sem("f_ln_done"), sem("f_t"), sem("f_t_moved")
        h_done, half_done, leaky_done, act_done, a_t, a_t_moved = (
            sem(n) for n in ("h_done", "half_done", "leaky_done", "act_done", "a_t", "a_t_moved"))
        negd_done, absd_done, expd_done, den_done, top_done = (
            sem(n) for n in ("negd_done", "absd_done", "expd_done", "den_done", "top_done"))
        y_psum, y_done, y_stored = sem("y_psum"), sem("y_done"), sem("y_stored")
        y_summed, count_init, passed = sem("y_summed"), sem("count_init"), sem("passed")
        scalar_left, vector_left = sem("scalar_left"), sem("vector_left")

        def has(b):
            return not isinstance(b, int) or 0 <= b < NB

        def iterations(eng, emit):
            for it in range(-3, 2):
                emit(it)
            with eng.Fori(2, NB - 4) as it:
                emit(it)
            for it in range(NB - 4, NB + 1):
                emit(it)

        def tiles(eng, emit):
            emit(0)
            with eng.Fori(1, NT) as i:
                emit(i)

        def score_head(it, s):
            return (it + 1, s + LEAD) if s < H - LEAD else (it + 2, s + LEAD - H)

        def guests(it, s):
            counts = [it + (s > 1), it + (s > 3), it + 3 + (s > 5), it - 1 + (s > 6)]
            if isinstance(it, int):
                return sum(min(max(n, 0), NB) for n in counts)
            return it * 4 + (2 + (s > 1) + (s > 3) + (s > 5) + (s > 6))

        def settled(eng):
            eng.sem_inc(passed, 1)

        block = outer.enter_context(nc.Block())

        @block.sync
        def _(sp):
            sp.dma_start(wr[:, :, :], w_router.partition_broadcast(P)).then_inc(wr_loaded, 16)

            def load_inputs(b):
                wait(sp, krest_done, b)
                wait(sp, k1_done, b)
                wait(sp, v_t, b)
                sp.dma_start(c_in[:, :], ctx_dh[b]).then_inc(c_loaded, 16)
                wait(sp, q_done, b)
                sp.dma_start(x_in[:, :], x_dh[b]).then_inc(x_loaded, 16)

            load_inputs(0)
            for kind, block_of in ((0, wfc_block), (1, wpr_block)):
                sp.dma_start(wst[kind][:, :], block_of(0)).then_inc(wst_loaded[kind], 16)

            def step(it):
                if has(it + 2):
                    b = it + 2
                    wait(sp, shifted, (b - RING + 1) * NQ * GH)
                    settled(sp)
                    wait(sp, k3_done, b + 1)
                    for n, part in enumerate(K_PART):
                        if part == 0:
                            wait(sp, k1_done, b + 1)
                        if part == 1:
                            wait(sp, k2_done, b + 1)
                        sp.dma_start(kst[n * DH:(n + 1) * DH, b % RING, :, :],
                                     kparts[:, part, :]).then_inc(k_stacked, 16)
                if has(it - 1):
                    wait(sp, mid_done, it - 1)
                    sp.dma_start(x_res[:, :], x[it - 1]).then_inc(res_loaded, 16)
                if has(it + 2):
                    wait(sp, q1_done, b + 1)
                    wait(sp, q2_done, b + 1)
                    wait(sp, q3_done, b + 1)
                    settled(sp)
                    for n, part in enumerate(Q_PART):
                        sp.dma_start(qst[n * DH:(n + 1) * DH, b % RING, :, :],
                                     qparts[:, part, :]).then_inc(q_stacked, 16)
                if has(it) and has(it + 1):
                    sp.wait_ge(w_t[0], it + 1)
                    sp.dma_start(wst[0][:, :], wfc_block(it + 1)).then_inc(wst_loaded[0], 16)
                if has(it):
                    sp.wait_ge(guest_read, guests(it, 4))
                    e, r, s = it // 16, (it // 4) % 4, it % 4
                    sp.dma_start(wproj_t[:, e, bass.ds(s * 4, 4), bass.ds(r * P, P)],
                                 wpr_out[:, :, :]).then_inc(wpr_stored, 16)
                    if has(it + 1):
                        sp.wait_ge(w_t[1], it + 1)
                        sp.dma_start(wst[1][:, :], wpr_block(it + 1)).then_inc(wst_loaded[1], 16)
                if has(it + 1):
                    b = it + 1
                    for n, made in ((0, c1_done), (1, c2_done)):
                        sp.wait_ge(made, b + 1)
                        sp.dma_start(qst[KR + n:KR + n + 1, b % RING, :, :],
                                     cparts[:, n, :]).then_inc(c_stacked, 16)
                if has(it + 4):
                    load_inputs(it + 4)

            iterations(sp, step)

            sp.wait_ge(scalar_left, 1)
            sp.wait_ge(vector_left, 1)
            sp.wait_ge(wpr_stored, 16 * NB)
            sp.wait_ge(scattered, 16 * NB)
            sp.wait_ge(padded, 16)
            sp.dma_start(rows_in[:, 0, :], sorted_rows[0:P, :]).then_inc(rows_loaded, 16)
            sp.wait_ge(rows_loaded, 16)
            sp.dma_start(rows_in[:, 1, :], sorted_rows[P:2 * P, :]).then_inc(rows_loaded, 16)
            for e in range(NE):
                for s in range(4):
                    sp.dma_start(wpr_sb[:, e, 4 * s:4 * s + 4, :],
                                 wproj_t[:, e, 4 * s:4 * s + 4, :]).then_inc(wpr_loaded, 16)
            with sp.Fori(2, NT) as i:
                sp.wait_ge(y_done, i - 1)
                settled(sp)
                sp.wait_ge(rows_loaded, 16 * i)
                settled(sp)
                sp.dma_start(rows_in[:, i % 2, :], sorted_rows[bass.ds(i * P, P), :]).then_inc(rows_loaded, 16)

        @block.gpsimd
        def _(pool):
            pool.memset(ident[:, :], 0.0).then_inc(const_a, 1)
            pool.memset(upper[:, :], 1.0).then_inc(const_a, 1)
            pool.memset(ones[:, :], 1.0).then_inc(const_ready, 1)
            pool.memset(neghalf[:, :], -0.5).then_inc(const_ready, 1)
            pool.wait_ge(const_a, 2)
            pool.affine_select(out=ident[:, :], in_=ident[:, :], compare_op=ALU.not_equal, fill=1.0, base=0,
                               pattern=[[-1, P]], channel_multiplier=1).then_inc(const_ready, 1)
            pool.affine_select(out=upper[:, :], in_=upper[:, :], compare_op=ALU.is_gt, fill=0.0, base=0,
                               pattern=[[1, P]], channel_multiplier=-1).then_inc(const_ready, 1)
            pool.iota(ident_i[:, :], pattern=[[0, 1]], base=0, channel_multiplier=1).then_inc(const_ready, 1)
            pool.iota(starts_i[:, :], pattern=[[P, NT]], base=0, channel_multiplier=0).then_inc(const_ready, 1)
            pool.wait_ge(const_ready, 6)

            def power(dst, var, tmp, have, mid, done, b):
                pool.wait_ge(have, b + 1)
                settled(pool)
                pool.tensor_scalar(tmp[:, :], var, EPS, None, ALU.add).then_inc(mid, 1)
                pool.wait_ge(mid, b + 1)
                pool.tensor_tensor(dst, tmp[:, :], neghalf[:, :], ALU.pow).then_inc(done, 1)

            def values(b, g):
                wait(pool, pv_done, NQ * (b - 1) + NCH * (g + 1))
                pool.wait_ge(guest_read, guests(b - 3, 6))
                pool.tensor_copy(vt[:, g * GH:(g + 1) * GH, :, 0:DH],
                                 vt_next[:, b % RING, g * GH:(g + 1) * GH, :, :]).then_inc(v_half[g], 1)

            def step(it):
                b = it + 3
                if has(it):
                    values(it, 1)
                if has(b):
                    pool.wait_ge(k1_done, b + 1)
                    wait(pool, k2_done, b)
                    pool.tensor_tensor(krest[:, :], c_in[:, :], kparts[:, 0, :], ALU.subtract).then_inc(krest_done, 1)
                    power(rstd1[:, :], mv1[:, 1:2], ve1, mv1_done, ve1_done, rstd1_done, b)
                if has(it - 1):
                    power(row[:, M + 1:M + 2], row[:, M + 1:M + 2], ve2, mv2_done, ve2_done, rstd2_done, it - 1)
                if has(b):
                    pool.wait_ge(k2_done, b + 1)
                    pool.wait_ge(krest_done, b + 1)
                    pool.tensor_tensor(kparts[:, 2, :], krest[:, :], kparts[:, 1, :], ALU.subtract).then_inc(k3_done, 1)
                if has(it + 1):
                    values(it + 1, 0)
                if has(b):
                    pool.wait_ge(q1_done, b + 1)
                    wait(pool, q2_done, b)
                    pool.tensor_tensor(qrest[:, :], qf[:, :], qparts[:, 0, :], ALU.subtract).then_inc(qrest_done, 1)
                    pool.wait_ge(q2_done, b + 1)
                    pool.wait_ge(qrest_done, b + 1)
                    pool.tensor_tensor(qparts[:, 2, :], qrest[:, :], qparts[:, 1, :], ALU.subtract).then_inc(q3_done, 1)
                if has(it - 1):
                    pool.wait_ge(slot_done, it)
                    pool.wait_ge(row_done, it)
                    settled(pool)
                    pool.indirect_dma_start(
                        out=sorted_rows[:, :], out_offset=bass.IndirectOffsetOnAxis(ap=slot[:, 0:1], axis=0),
                        in_=row[:, :], in_offset=None).then_inc(scattered, 16)

            iterations(pool, step)
            pool.wait_ge(pad_done, 1)
            pool.indirect_dma_start(
                out=sorted_rows[:, :], out_offset=bass.IndirectOffsetOnAxis(ap=pad_slot[:, 0:1], axis=0),
                in_=pad_row[:, :], in_offset=None).then_inc(padded, 16)

            with pool.Fori(0, NT) as i:
                pool.wait_ge(y_done, i + 1)
                settled(pool)
                pool.indirect_dma_start(
                    out=out[:, :], out_offset=bass.IndirectOffsetOnAxis(ap=y_token[:, 0:1], axis=0),
                    in_=y_out[:, :], in_offset=None, bounds_check=NTOK - 1, oob_is_err=False).then_inc(y_stored, 16)
            pool.wait_ge(y_stored, 16 * NT)

        @block.scalar
        def _(sc):
            def exps(b, q):
                for hh in range(GH):
                    n = (b * NQ + q) * GH + hh
                    sc.wait_ge(shifted, n + 1)
                    if hh == 0:
                        wait(sc, pv_done, b * NQ + q - 3)
                    nc.scalar.activation(probs[:, q % 4, hh, :], st_bank[hh % 2][:, :], ACT.Exp,
                                         scale=SCALE).then_inc(exped, 1)

            def step(it):
                b = it + 3
                for s in range(NQ):
                    if s == 0 and has(it - 1):
                        o_evac(it - 1, 1)
                    if s == 4 and has(it):
                        o_evac(it, 0)
                    if s < NQ - 1 and has(it):
                        exps(it, s + 1)
                    if s == NQ - 1 and has(it + 1):
                        exps(it + 1, 0)
                    if s == 1 and has(it):
                        sc.wait_ge(w_t[0], it + 1)
                        nc.scalar.activation(wfc_sb[:, it // 16, :, bass.ds((it % 16) * P, P)],
                                             st_bank[0][:, :].rearrange("p (k n) -> p k n", k=KC),
                                             ACT.Copy).then_inc(guest_read, 1)
                    if s == 2 and has(b):
                        sc.wait_ge(c_loaded, 16 * (b + 1))
                        wait(sc, k_stacked, 16 * SPLIT * b)
                        nc.scalar.activation(kparts[:, 0, :], c_in[:, :], ACT.Copy).then_inc(k1_done, 1)
                    if s == 3 and has(it):
                        sc.wait_ge(w_t[1], it + 1)
                        wait(sc, wpr_stored, 16 * it)
                        nc.scalar.activation(wpr_out[:, :, :],
                                             st_bank[0][:, :].rearrange("p (k n) -> p k n", k=NCH),
                                             ACT.Copy).then_inc(guest_read, 1)
                    if s == 4 and has(b):
                        sc.wait_ge(krest_done, b + 1)
                        nc.scalar.activation(kparts[:, 1, :], krest[:, :], ACT.Copy).then_inc(k2_done, 1)
                    if s == 5 and has(b):
                        sc.wait_ge(v_t, b + 1)
                        wait(sc, v_half[1], b - RING + 1)
                        nc.scalar.activation(
                            vt_next[:, b % RING, :, :, :].rearrange("p h c d -> p c h d"),
                            st_bank[0][:, :].rearrange("p (c d h) -> p c h d", c=NCH, h=H),
                            ACT.Copy).then_inc(guest_read, 1)
                    if s == 5 and has(b):
                        sc.wait_ge(q_done, b + 1)
                        wait(sc, q_stacked, 16 * SPLIT * b)
                        nc.scalar.activation(qparts[:, 0, :], qf[:, :], ACT.Copy).then_inc(q1_done, 1)
                    if s == 6 and has(it - 1):
                        sc.wait_ge(ranked, it)
                        wait(sc, count_done, it - 1)
                        nc.scalar.activation(ranks[:, :], st_bank[0][:, 0:2], ACT.Copy).then_inc(guest_read, 1)
                    if s == 7 and has(b):
                        sc.wait_ge(qrest_done, b + 1)
                        nc.scalar.activation(qparts[:, 1, :], qrest[:, :], ACT.Copy).then_inc(q2_done, 1)

            def o_evac(b, g):
                sc.wait_ge(pv_done, NQ * b + NCH * (g + 1))
                wait(sc, o_t[g], b)
                nc.scalar.activation(o_sb[:, g, :], o_bank[:, :], ACT.Copy).then_inc(o_moved[g], 1)

            iterations(sc, step)
            nc.scalar.activation(left_mark[:, :], neghalf[:, :], ACT.Copy).then_inc(scalar_left, 1)
            sc.wait_ge(vector_left, 1)

            def tile(i):
                sc.wait_ge(absd_done, i + 1)
                nc.scalar.activation(expd[:, :], absd[:, :], ACT.Exp, scale=-1.0).then_inc(expd_done, 1)
                for hs in range(HS):
                    n = i * HS + hs
                    sc.wait_ge(h_done, n + 1)
                    nc.scalar.activation(half_h[:, hs % 2, :], h_bank[hs % 2][:, :], ACT.Copy,
                                         scale=0.5).then_inc(half_done, 1)
                    sc.wait_ge(leaky_done, n + 1)
                    wait(sc, a_t, n - 1)
                    nc.scalar.activation(act[:, hs % 2, :], leaky[:, hs % 2, :], ACT.Square).then_inc(act_done, 1)

            tiles(sc, tile)

        @block.tensor
        def _(pe):
            pe.wait_ge(const_ready, 6)
            pe.wait_ge(v_const, 2)

            def transposed(b, src, dst, done):
                for k in range(NCH):
                    last = nc.tensor.transpose(dst[:, k * P:(k + 1) * P], src[:, k * P:(k + 1) * P], ident[:, :])
                last.then_inc(done, 1)

            def score(b, h, j):
                n = (b * H + h) * 2 + j // 2
                if h == 0 and j == 0:
                    pe.wait_ge(k_stacked, 16 * SPLIT * (b + 1))
                    pe.wait_ge(q_stacked, 16 * SPLIT * (b + 1))
                if j % 2 == 0:
                    wait(pe, maxed, n - 1)
                last = nc.tensor.matmul(s_pair[j // 2][:, j % 2, :], qst[0:KR, b % RING, h, j * P:(j + 1) * P],
                                        kst[0:KR, b % RING, h, :], start=True, stop=True)
                if j % 2 == 1:
                    last.then_inc(scored, 1)

            def shift(it, s, b, q, hh):
                n = (b * NQ + q) * GH + hh
                h, c = (q // NCH) * GH + hh, q % NCH
                if q == 0 and hh == 0:
                    pe.wait_ge(c_stacked, 32 * (b + 1))
                wait(pe, exped, n - 1)
                if hh == 0:
                    wait(pe, guest_read, guests(it, s))
                nc.tensor.matmul(st_bank[hh % 2][:, :], kst[0:KR + 2, b % RING, h, c * P:(c + 1) * P],
                                 qst[0:KR + 2, b % RING, h, :], start=True, stop=True).then_inc(shifted, 1)

            def product(b, q):
                g, c = q // NCH, q % NCH
                pe.wait_ge(exped, (b * NQ + q + 1) * GH)
                if c == 0:
                    pe.wait_ge(v_half[g], b + 1)
                    if g == 0:
                        wait(pe, o_moved[1], b)
                    else:
                        pe.wait_ge(o_moved[0], b + 1)
                for hh in range(GH):
                    last = nc.tensor.matmul(o_bank[32 * hh:32 * hh + 32, :], vt[:, g * GH + hh, c, :],
                                            probs[:, q % 4, hh, :], start=(c == 0), stop=(c == NCH - 1))
                last.then_inc(pv_done, 1)

            def guest(it, s):
                if (s == 1 or s == 3) and has(it):
                    w = s // 2
                    pe.wait_ge(wst_loaded[w], 16 * (it + 1))
                    bank_clear(it, s)
                    transposed(it, wst[w], st_bank[0], w_t[w])
                if s == 5 and has(it + 3):
                    pe.wait_ge(c_loaded, 16 * (it + 4))
                    bank_clear(it, s)
                    transposed(it + 3, c_in, st_bank[0], v_t)
                if s == 6 and has(it - 1):
                    pe.wait_ge(one_done, it)
                    bank_clear(it, s)
                    nc.tensor.matmul(st_bank[0][:, 0:1], upper[:, :], to_one[:, :], start=True, stop=True)
                    nc.tensor.matmul(st_bank[0][:, 1:2], ones[:, :], to_one[:, :], start=True,
                                     stop=True).then_inc(ranked, 1)

            def bank_clear(it, s):
                n = (it * NQ + s + 1) * GH
                wait(pe, exped, made_tiles(n + 3))
                wait(pe, guest_read, guests(it, s))

            def made_tiles(n):
                return min(n, NB * NQ * GH) if isinstance(n, int) else n

            def made(n):
                return min(n, NB) if isinstance(n, int) else n

            def step(it):
                for s in range(NQ):
                    sb_, sh = score_head(it, s)
                    tb, tq = (it, s + 1) if s < NQ - 1 else (it + 1, 0)
                    for j in range(NCH):
                        if has(tb):
                            shift(it, s, tb, tq, j)
                        if has(sb_):
                            score(sb_, sh, j)
                    guest(it, s)
                    if has(it):
                        product(it, s)
                    if s == 0 and has(it - 1):
                        pe.wait_ge(o_moved[1], it)
                        pe.wait_ge(o_normed[0], it)
                        transposed(it - 1, o_sb[:, 1, :], m_bank, o_t[1])
                    if s == 2 and has(it - 1):
                        pe.wait_ge(o_normed[1], it)
                        for k in range(NCH):
                            last = nc.tensor.transpose(m_bank[:, k * P:(k + 1) * P], o_norm[:, k, :], ident[:, :])
                        last.then_inc(o_back, 1)
                    if s == 4 and has(it + 1):
                        pe.wait_ge(maxed, (it + 2) * H * 2)
                        pe.wait_ge(head_copied, it + 2)
                        wait(pe, mid_done, it)
                        nc.tensor.transpose(m_bank[0:H * NCH, 0:P], maxes[:, :], ident[:, :]).then_inc(max_t, 1)
                    if s == 6 and has(it):
                        pe.wait_ge(o_moved[0], it + 1)
                        wait(pe, crest_done, made(it + 2))
                        wait(pe, mid_done, it)
                        transposed(it, o_sb[:, 0, :], m_bank, o_t[0])

            iterations(pe, step)

            pe.wait_ge(scalar_left, 1)
            pe.wait_ge(vector_left, 1)
            pe.wait_ge(table_done, 1)

            def flip(i):
                pe.wait_ge(f_ln_done, i + 1)
                wait(pe, f_t_moved, i)
                transposed(i, f_ln, xt_bank, f_t)

            def tile(i, more=True):
                e = pe.value_load(expert_of[0:1, bass.ds(i, 1)], min_val=0, max_val=NE - 1)

                def up(hs):
                    n = i * HS + hs
                    wait(pe, leaky_done, n - 1)
                    for k in range(KC):
                        last = nc.tensor.matmul(h_bank[hs % 2][:, :], f_lnt[:, k, :],
                                                wfc_sb[:, e, k, hs * 512:(hs + 1) * 512],
                                                start=(k == 0), stop=(k == KC - 1))
                    last.then_inc(h_done, 1)

                def turn(hs):
                    n = i * HS + hs
                    pe.wait_ge(act_done, n + 1)
                    wait(pe, a_t_moved, n - 1)
                    transposed(i, act[:, hs % 2, :], at_bank[hs % 2], a_t)

                def down(hs):
                    pe.wait_ge(a_t_moved, i * HS + hs + 1)
                    if hs == 0:
                        wait(pe, y_done, i)
                    for k in range(4 * hs, 4 * hs + 4):
                        last = nc.tensor.matmul(y_bank[:, :], act_t[:, k, :], wpr_sb[:, e, k, :],
                                                start=(k == 0), stop=(k == HID // P - 1))
                    if hs == HS - 1:
                        last.then_inc(y_psum, 1)

                pe.wait_ge(f_t_moved, i + 1)
                up(0)
                up(1)
                turn(0)
                up(2)
                turn(1)
                up(3)
                turn(2)
                if isinstance(i, int) and i == 0:
                    pe.wait_ge(wpr_loaded, 16 * 4 * NE)
                down(0)
                turn(3)
                down(1)
                if more:
                    flip(i + 1)
                down(2)
                down(3)

            flip(0)
            tile(0)
            with pe.Fori(1, NT - 1) as i:
                tile(i)
            tile(NT - 1, more=False)

        @block.vector
        def _(dve):
            nc.vector.memset(kst[KR:KR + 2, :, :, :], 1.0).then_inc(v_const, 1)
            nc.vector.memset(vt[:, :, :, DH:2 * DH], 1.0).then_inc(v_const, 1)
            nc.vector.memset(count1[:, :], 0.0).then_inc(count_init, 1)
            nc.vector.memset(pad_row[:, :], 0.0).then_inc(pad_a, 1)
            dve.wait_ge(const_ready, 6)
            nc.vector.tensor_copy(token[:, :], ident_i[:, :]).then_inc(count_init, 1)
            nc.vector.tensor_copy(starts[:, :], starts_i[:, :]).then_inc(table_a, 1)
            dve.wait_ge(wr_loaded, 16)
            nc.vector.tensor_tensor(wdiff[:, :], wr[:, 1, :], wr[:, 0, :], ALU.subtract).then_inc(wdiff_ready, 1)
            dve.wait_ge(count_init, 2)
            dve.wait_ge(wdiff_ready, 1)

            def norm(b, g):
                dve.wait_ge(o_t[g], b + 1)
                got = m_bank[:, :].rearrange("p (j h r) -> p j h r", j=NCH, h=GH)
                nc.vector.reciprocal(rsum[:, :, :], got[:, :, :, DH]).then_inc(rsum_done[g], 1)
                dve.wait_ge(rsum_done[g], b + 1)
                nc.vector.tensor_tensor(
                    o_norm[:, :, g * GH * DH:(g + 1) * GH * DH].rearrange("p j (h r) -> p j h r", h=GH),
                    got[:, :, :, 0:DH], rsum[:, :, :].unsqueeze(3).to_broadcast([P, NCH, GH, DH]),
                    ALU.mult).then_inc(o_normed[g], 1)

            def maxima(b, h, pair):
                dst = max_head if h < LEAD else maxes
                dve.wait_ge(scored, (b * H + h) * 2 + pair + 1)
                nc.vector.reduce_max(dst[:, h * NCH + 2 * pair:h * NCH + 2 * pair + 2], s_pair[pair][:, :, :],
                                     AX.X).then_inc(maxed, 1)

            def step(it):
                b = it + 3
                for s in range(NQ):
                    if s == 0 and has(it + 1):
                        wait(dve, max_t, it + 1)
                        dve.wait_ge(maxed, (it + 1) * H * 2 + LEAD * 2)
                        nc.vector.tensor_copy(maxes[:, 0:LEAD * NCH], max_head[:, :]).then_inc(head_copied, 1)
                        dve.wait_ge(head_copied, it + 2)
                    sb_, sh = score_head(it, s)
                    if has(sb_):
                        maxima(sb_, sh, 0)
                    if s == 1 and has(it - 1):
                        norm(it - 1, 1)
                    if s == 2 and has(b):
                        dve.wait_ge(x_loaded, 16 * (b + 1))
                        nc.vector.bn_stats(stats1[:, :], x_in[:, :]).then_inc(stats1_done, 1)
                        dve.wait_ge(stats1_done, b + 1)
                        wait(dve, ve1_done, b)
                        settled(dve)
                        nc.vector.bn_aggr(mv1[:, :], stats1[:, :]).then_inc(mv1_done, 1)
                    if s == 3 and has(it - 1):
                        middle(it - 1)
                    if s == 4 and has(b):
                        dve.wait_ge(rstd1_done, b + 1)
                        wait(dve, q1_done, b)
                        wait(dve, qrest_done, b)
                        nc.vector.tensor_scalar(qf[:, :], x_in[:, :], mv1[:, 0:1], rstd1[:, 0:1], ALU.subtract,
                                                ALU.mult).then_inc(q_done, 1)
                    if s == 5 and has(it + 1):
                        shifts(it + 1)
                    if s == 7 and has(it):
                        norm(it, 0)
                    if has(sb_):
                        maxima(sb_, sh, 1)
                    if s == 5 and has(it - 1):
                        route(it - 1)
                    if s == 7 and has(it - 1):
                        place(it - 1)

            def middle(b):
                dve.wait_ge(o_back, b + 1)
                dve.wait_ge(res_loaded, 16 * (b + 1))
                wait(dve, scattered, 16 * b)
                nc.vector.tensor_tensor(row[:, 0:M], m_bank[:, :], x_res[:, :], ALU.add).then_inc(mid_done, 1)
                dve.wait_ge(mid_done, b + 1)
                nc.vector.bn_stats(stats2[:, :], row[:, 0:M]).then_inc(stats2_done, 1)
                dve.wait_ge(stats2_done, b + 1)
                settled(dve)
                nc.vector.bn_aggr(row[:, M:M + 2], stats2[:, :]).then_inc(mv2_done, 1)

            def route(b):
                dve.wait_ge(rstd2_done, b + 1)
                nc.vector.tensor_scalar(xln[:, :], row[:, 0:M], row[:, M:M + 1], row[:, M + 1:M + 2], ALU.subtract,
                                        ALU.mult).then_inc(xln_done, 1)
                dve.wait_ge(xln_done, b + 1)
                nc.vector.tensor_tensor_reduce(out=prod[:, :], in0=xln[:, :], in1=wdiff[:, :], scale=1.0,
                                               scalar=0.0, op0=ALU.mult, op1=ALU.add,
                                               accum_out=row[:, M + 2:M + 3]).then_inc(ldiff_done, 1)
                dve.wait_ge(ldiff_done, b + 1)
                wait(dve, ranked, b)
                nc.vector.tensor_scalar(to_one[:, :], row[:, M + 2:M + 3], 0.0, None, ALU.is_gt).then_inc(one_done, 1)

            def shifts(b):
                dve.wait_ge(max_t, b + 1)
                wait(dve, c_stacked, 32 * b)
                top = m_bank[0:H * NCH, 0:P]
                nc.vector.tensor_scalar(cparts[:, 0, :], top, -1.0, None, ALU.mult).then_inc(c1_done, 1)
                dve.wait_ge(c1_done, b + 1)
                nc.vector.scalar_tensor_tensor(out=crest[:, :], in0=top, scalar=-1.0, in1=cparts[:, 0, :],
                                               op0=ALU.mult, op1=ALU.subtract).then_inc(crest_done, 1)
                dve.wait_ge(crest_done, b + 1)
                nc.vector.tensor_copy(cparts[:, 1, :], crest[:, :]).then_inc(c2_done, 1)

            def place(b):
                dve.wait_ge(guest_read, guests(b + 1, 7))
                wait(dve, token_done, b)
                wait(dve, count_done, b)
                nc.vector.scalar_tensor_tensor(out=neg_a[:, :], in0=ranks[:, 0:1], scalar=count1[:, 0:1],
                                               in1=token[:, :], op0=ALU.add, op1=ALU.subtract).then_inc(nega_done, 1)
                nc.vector.scalar_tensor_tensor(out=neg_b[:, :], in0=token[:, :], scalar=float(CAP - 1),
                                               in1=to_one[:, :], op0=ALU.subtract, op1=ALU.mult).then_inc(negb_done, 1)
                dve.wait_ge(nega_done, b + 1)
                dve.wait_ge(negb_done, b + 1)
                nc.vector.scalar_tensor_tensor(out=slot[:, :], in0=neg_a[:, :], scalar=-1.0, in1=neg_b[:, :],
                                               op0=ALU.mult, op1=ALU.subtract).then_inc(slot_done, 1)
                nc.vector.tensor_copy(row[:, M + 3:M + 4].bitcast(I32), token[:, :]).then_inc(row_done, 1)
                nc.vector.tensor_scalar(token[:, :], token[:, :], float(P), None, ALU.add).then_inc(token_done, 1)
                nc.vector.tensor_tensor(count1[:, :], count1[:, :], ranks[:, 1:2], ALU.add).then_inc(count_done, 1)

            iterations(dve, step)

            dve.wait_ge(pad_a, 1)
            dve.wait_ge(count_done, NB)
            nc.vector.memset(pad_row[:, M + 3:M + 4].bitcast(I32), NTOK).then_inc(pad_a, 1)
            nc.vector.tensor_scalar(pad_f[:, :], count1[:, :], -1.0, float(NTOK), ALU.mult, ALU.add).then_inc(pad_a, 1)
            dve.wait_ge(pad_a, 3)
            nc.vector.tensor_tensor(pad_slot[:, :], pad_f[:, :], ident_i[:, :], ALU.add).then_inc(pad_done, 1)
            dve.wait_ge(table_a, 1)
            nc.vector.tensor_scalar(expert_of[:, :], starts[:, :], pad_f[0:1, 0:1], None, ALU.is_gt).then_inc(table_done, 1)
            dve.wait_ge(padded, 16)
            nc.vector.tensor_copy(left_mark2[:, :], neghalf[:, :]).then_inc(vector_left, 1)
            dve.wait_ge(scalar_left, 1)

            def normalise(i):
                dve.wait_ge(rows_loaded, 16 * (i + 1))
                wait(dve, f_t, i)
                nc.vector.tensor_scalar(f_ln[:, :], rows_in[:, i % 2, 0:M], rows_in[:, i % 2, M:M + 1],
                                        rows_in[:, i % 2, M + 1:M + 2], ALU.subtract,
                                        ALU.mult).then_inc(f_ln_done, 1)
                wait(dve, absd_done, i)
                nc.vector.tensor_scalar(negd[:, :], rows_in[:, i % 2, M + 2:M + 3], -1.0, None,
                                        ALU.mult).then_inc(negd_done, 1)
                dve.wait_ge(negd_done, i + 1)
                wait(dve, expd_done, i)
                nc.vector.tensor_tensor(absd[:, :], rows_in[:, i % 2, M + 2:M + 3], negd[:, :],
                                        ALU.max).then_inc(absd_done, 1)

            def take(i):
                dve.wait_ge(f_t, i + 1)
                wait(dve, h_done, HS * i)
                nc.vector.tensor_copy(f_lnt[:, :, :], xt_bank[:, :].rearrange("p (k n) -> p k n", k=KC)).then_inc(f_t_moved, 1)

            def tile(i, more=True):
                def leak(hs):
                    n = i * HS + hs
                    dve.wait_ge(half_done, n + 1)
                    wait(dve, act_done, n - 1)
                    nc.vector.tensor_tensor(leaky[:, hs % 2, :], h_bank[hs % 2][:, :], half_h[:, hs % 2, :],
                                            ALU.max).then_inc(leaky_done, 1)

                def turned(hs):
                    dve.wait_ge(a_t, i * HS + hs + 1)
                    wait(dve, y_psum, i)
                    nc.vector.tensor_copy(act_t[:, 4 * hs:4 * hs + 4, :],
                                          at_bank[hs % 2][:, :].rearrange("p (k n) -> p k n", k=4)).then_inc(a_t_moved, 1)

                dve.wait_ge(expd_done, i + 1)
                nc.vector.tensor_scalar(den[:, :], expd[:, :], 1.0, None, ALU.add).then_inc(den_done, 1)
                dve.wait_ge(den_done, i + 1)
                nc.vector.reciprocal(top_w[:, :], den[:, :]).then_inc(top_done, 1)
                leak(0)
                leak(1)
                turned(0)
                leak(2)
                turned(1)
                leak(3)
                turned(2)
                if more:
                    normalise(i + 1)
                turned(3)
                if more:
                    take(i + 1)
                dve.wait_ge(y_psum, i + 1)
                dve.wait_ge(top_done, i + 1)
                wait(dve, y_stored, 16 * i)
                nc.vector.scalar_tensor_tensor(out=y_out[:, :], in0=y_bank[:, :], scalar=top_w[:, 0:1],
                                               in1=rows_in[:, i % 2, 0:M], op0=ALU.mult,
                                               op1=ALU.add).then_inc(y_summed, 1)
                nc.vector.tensor_copy(y_token[:, :], rows_in[:, i % 2, M + 3:M + 4].bitcast(I32)).then_inc(y_done, 1)

            normalise(0)
            take(0)
            tile(0)
            with dve.Fori(1, NT - 1) as i:
                tile(i)
            tile(NT - 1, more=False)


_INS = ["x", "ctx_2048", "L0_ffn_w_router", "L0_ffn_w_fc", "L0_ffn_w_proj"]


def kernel(**inputs):
    import concourse.bacc as bacc
    import numpy as np
    from concourse import mybir as _mybir
    from concourse.bass_utils import run_bass_kernel_spmd

    nc = bacc.Bacc("TRN2", target_bir_lowering=False, num_devices=1)
    arrays, args = {}, []
    for name in _INS:
        a = np.ascontiguousarray(inputs[name])
        arrays[f"in_{name}"] = a
        args.append(nc.dram_tensor(f"in_{name}", a.shape, _mybir.dt.from_np(a.dtype), kind="ExternalInput").ap())
    batches, rows, feats = inputs["x"].shape
    out = nc.dram_tensor("out", (batches * rows, feats), _mybir.dt.float32, kind="ExternalOutput").ap()
    build_program(nc, *args, out)
    r = run_bass_kernel_spmd(nc, [arrays], core_ids=[0])
    return r.results[0]["out"].reshape(batches, rows, feats)
```

```python
from contextlib import ExitStack

import concourse.bass as bass
from concourse import mybir

ALU = mybir.AluOpType
ACT = mybir.ActivationFunctionType
AX = mybir.AxisListType
F32 = mybir.dt.float32
BF16 = mybir.dt.bfloat16
I32 = mybir.dt.int32
F32R = mybir.dt.float32r

P = 128


def wait(eng, sem, value):
    if not isinstance(value, int) or value > 0:
        eng.wait_ge(sem, value)


def build_program(nc, x, ctx, w_router, w_fc, w_proj, out):
    NB, D, M = x.shape
    H = 8
    DH = D // H
    NCH = M // P
    GH = 4
    NG = H // GH
    NQ = NG * NCH
    NE, HID, _ = w_fc.shape
    NTOK = NB * D
    CAP = NTOK + P
    NT = CAP // P
    KC = M // P
    HH = HID // 2
    HS = HH // 512
    HC = HH // P
    HI, LO = 0, 1
    ROW = M + 4
    LEAD = 4
    SPLIT = 6
    KR = SPLIT * DH
    EPS = 1e-5
    SCALE = 1.0 / float(DH) ** 0.5
    RING = 3
    K_PART = [0, 1, 0, 1, 2, 0]
    Q_PART = [0, 0, 1, 1, 0, 2]
    assert D == P and M == 512 and NQ == H and NB == NE * HID // P

    sorted_rows = nc.dram_tensor("sorted_rows", (CAP, ROW), F32, kind="Internal").ap()
    partial = nc.dram_tensor("partial", (CAP, M), F32, kind="Internal").ap()
    up_t = nc.dram_tensor("up_t", (2, P, NE, 2, KC, HH), F32, kind="Internal").ap()
    down_t = nc.dram_tensor("down_t", (2, P, NE, 2, HC, M), F32, kind="Internal").ap()
    x_dh = x.rearrange("b (h d) m -> b d h m", d=DH)
    ctx_dh = ctx.rearrange("b (h d) m -> b d h m", d=DH)
    wfc_rows = w_fc.rearrange("e (r p) d -> (e r) p d", p=P)
    wpr_rows = w_proj.rearrange("e (r p) n -> (e r) p n", p=P)

    def wfc_block(n):
        return wfc_rows[(n // 8) % 2 * (HID // P) + n // 16 * HC + n % 8]

    def wpr_block(n):
        return wpr_rows[n // 4, :, bass.ds((n % 4) * 512, 512)]

    with ExitStack() as outer:
        def sem(name):
            return outer.enter_context(nc.semaphore(name))

        def psum(name, shape):
            return outer.enter_context(nc.psum_tensor(name, shape, F32))

        def keep(name, shape, dt):
            return outer.enter_context(nc.sbuf_tensor(name, shape, dt))

        s_pair = [psum("s_pair0", [P, 2, 512]), psum("s_pair1", [P, 2, 512])]
        st_bank = [psum("st_bank0", [P, 512]), psum("st_bank1", [P, 512])]
        o_bank, m_bank = psum("o_bank", [P, 512]), psum("m_bank", [P, 512])

        ident = keep("ident", [P, P], F32)
        left_mark = keep("left_mark", [P, 1], F32)
        left_mark2 = keep("left_mark2", [P, 1], F32)
        neghalf = keep("neghalf", [P, 1], F32)
        expert_of = keep("expert_of", [1, NT], I32)
        up_sb = keep("up_sb", [P, NE, 2, KC, HH], F32R)

        inner = ExitStack()

        def sb(name, shape, dt):
            return inner.enter_context(nc.sbuf_tensor(name, shape, dt))

        kst = sb("kst", [P, RING, H, M], BF16)
        qst = sb("qst", [P, RING, H, M], BF16)
        probs = sb("probs", [P, 4, GH, M], F32)
        x_in = sb("x_in", [P, M], F32)
        c_in = sb("c_in", [P, M], F32)
        x_res = sb("x_res", [P, M], F32)
        kparts = sb("kparts", [P, 3, M], BF16)
        qparts = sb("qparts", [P, 3, M], BF16)
        krest = sb("krest", [P, M], F32)
        qrest = sb("qrest", [P, M], F32)
        qf = sb("qf", [P, M], F32)
        vt = sb("vt", [P, H, NCH, 2 * DH], F32)
        vt_next = sb("vt_next", [P, RING, H, NCH, DH], F32)
        max_head = sb("max_head", [P, LEAD * NCH], F32)
        maxes = sb("maxes", [P, H * NCH], F32)
        cparts = sb("cparts", [H * NCH, 2, P], BF16)
        crest = sb("crest", [H * NCH, P], F32)
        o_sb = sb("o_sb", [P, NG, M], F32)
        o_norm = sb("o_norm", [P, NCH, D], F32)
        rsum = sb("rsum", [P, NCH, GH], F32)
        row = sb("row", [P, ROW], F32)
        weighted = sb("weighted", [P, M], F32)
        wdiff = sb("wdiff", [P, M], F32)
        stats1 = sb("stats1", [P, 6], F32)
        mv1 = sb("mv1", [P, 2], F32)
        ve1 = sb("ve1", [P, 1], F32)
        rstd1 = sb("rstd1", [P, 1], F32)
        stats2 = sb("stats2", [P, 6], F32)
        ve2 = sb("ve2", [P, 1], F32)
        to_one = sb("to_one", [P, 1], BF16)
        upper = sb("upper", [P, P], BF16)
        ones = sb("ones", [P, P], BF16)
        count1 = sb("count1", [P, 1], F32)
        ident_i = sb("ident_i", [P, 1], I32)
        token = sb("token", [P, 1], F32)
        neg_a = sb("neg_a", [P, 1], F32)
        neg_b = sb("neg_b", [P, 1], F32)
        ranks = sb("ranks", [P, 2], F32)
        slot = sb("slot", [P, 1], I32)
        pad_row = sb("pad_row", [P, ROW], F32)
        pad_slot = sb("pad_slot", [P, 1], I32)
        pad_f = sb("pad_f", [P, 1], F32)
        starts_i = sb("starts_i", [1, NT], I32)
        starts = sb("starts", [1, NT], F32)
        wst = [sb("wst0", [P, 512], F32), sb("wst1", [P, 512], F32)]
        w_raw = [sb("w_raw0", [P, NCH, P], F32), sb("w_raw1", [P, NCH, P], F32)]
        w_hi = [sb("w_hi0", [P, NCH, P], F32R), sb("w_hi1", [P, NCH, P], F32R)]
        w_lo = [sb("w_lo0", [P, NCH, P], F32R), sb("w_lo1", [P, NCH, P], F32R)]
        inner.close()

        second = outer.enter_context(ExitStack())

        def sb2(name, shape, dt):
            return second.enter_context(nc.sbuf_tensor(name, shape, dt))

        down_sb = sb2("down_sb", [P, NE, 2, HC, M], F32R)
        part_in = sb2("part_in", [P, 3, M], F32)
        rows_in = sb2("rows_in", [P, 3, ROW], F32)
        f_ln = sb2("f_ln", [P, M], F32)
        f_lnt = sb2("f_lnt", [P, 2, KC, P], F32R)
        half_h = sb2("half_h", [P, 2, 512], F32)
        leaky = sb2("leaky", [P, 2, 512], F32)
        act = sb2("act", [P, 2, 512], F32)
        act_t = sb2("act_t", [P, 2, HC, P], F32R)
        absd = sb2("absd", [P, 1], F32)
        negd = sb2("negd", [P, 1], F32)
        expd = sb2("expd", [P, 1], F32)
        den = sb2("den", [P, 1], F32)
        top_w = sb2("top_w", [P, 1], F32)
        y_out = sb2("y_out", [P, M], F32)
        y_token = sb2("y_token", [P, 1], I32)

        h_bank = [s_pair[0][:, 0, :], s_pair[1][:, 0, :]]
        at_bank, y_bank, xt_bank = st_bank, o_bank, m_bank

        x_loaded, c_loaded, res_loaded = sem("x_loaded"), sem("c_loaded"), sem("res_loaded")
        wr_loaded = sem("wr_loaded")
        wst_loaded = [sem("wst_loaded0"), sem("wst_loaded1")]
        const_a, const_ready = sem("const_a"), sem("const_ready")
        v_const = sem("v_const")
        wdiff_ready = sem("wdiff_ready")
        k1_done, krest_done, k2_done, k3_done = (sem(n) for n in ("k1_done", "krest_done", "k2_done", "k3_done"))
        q1_done, qrest_done, q2_done, q3_done = (sem(n) for n in ("q1_done", "qrest_done", "q2_done", "q3_done"))
        stats1_done, mv1_done, ve1_done, rstd1_done, q_done = (
            sem(n) for n in ("stats1_done", "mv1_done", "ve1_done", "rstd1_done", "q_done"))
        k_stacked, q_stacked = sem("k_stacked"), sem("q_stacked")
        scored, maxed, head_copied = sem("scored"), sem("maxed"), sem("head_copied")
        max_t, c1_done, crest_done, c2_done, c_stacked = (
            sem(n) for n in ("max_t", "c1_done", "crest_done", "c2_done", "c_stacked"))
        shifted, exped, pv_done = sem("shifted"), sem("exped"), sem("pv_done")
        v_t, v_half = sem("v_t"), [sem("v_half0"), sem("v_half1")]
        o_moved = [sem("o_moved0"), sem("o_moved1")]
        o_t = [sem("o_t0"), sem("o_t1")]
        rsum_done = [sem("rsum_done0"), sem("rsum_done1")]
        o_normed = [sem("o_normed0"), sem("o_normed1")]
        o_back, mid_done = sem("o_back"), sem("mid_done")
        stats2_done, mv2_done, ve2_done, rstd2_done = (
            sem(n) for n in ("stats2_done", "mv2_done", "ve2_done", "rstd2_done"))
        ldiff_done, one_done, ranked, nega_done, negb_done = (
            sem(n) for n in ("ldiff_done", "one_done", "ranked", "nega_done", "negb_done"))
        slot_done, count_done, token_done, row_done, scattered = (
            sem(n) for n in ("slot_done", "count_done", "token_done", "row_done", "scattered"))
        guest_read = sem("guest_read")
        pad_a, pad_done, table_a, table_done, padded = (
            sem(n) for n in ("pad_a", "pad_done", "table_a", "table_done", "padded"))
        w_t = [sem("w_t0"), sem("w_t1")]
        w_rounded = [sem("w_rounded0"), sem("w_rounded1")]
        w_split = [sem("w_split0"), sem("w_split1")]
        w_stored = [sem("w_stored0"), sem("w_stored1")]
        up_loaded = [sem("up_loaded0"), sem("up_loaded1")]
        down_loaded = [sem("down_loaded0"), sem("down_loaded1")]
        rows_loaded, part_loaded, part_stored = sem("rows_loaded"), sem("part_loaded"), sem("part_stored")
        f_hi_done, a_hi_done = sem("f_hi_done"), sem("a_hi_done")
        f_ln_done, f_t, f_t_moved = sem("f_ln_done"), sem("f_t"), sem("f_t_moved")
        h_done, half_done, leaky_done, act_done, a_t, a_t_moved = (
            sem(n) for n in ("h_done", "half_done", "leaky_done", "act_done", "a_t", "a_t_moved"))
        negd_done, absd_done, expd_done, den_done, top_done = (
            sem(n) for n in ("negd_done", "absd_done", "expd_done", "den_done", "top_done"))
        y_psum, y_done, y_stored = sem("y_psum"), sem("y_done"), sem("y_stored")
        y_summed, count_init, passed = sem("y_summed"), sem("count_init"), sem("passed")
        scalar_left, vector_left = sem("scalar_left"), sem("vector_left")

        def has(b):
            return not isinstance(b, int) or 0 <= b < NB

        def iterations(eng, emit):
            for it in range(-3, 2):
                emit(it)
            with eng.Fori(2, NB - 4) as it:
                emit(it)
            for it in range(NB - 4, NB + 1):
                emit(it)

        def tiles(eng, emit, after_first=None):
            for p in range(2):
                emit(p * NT)
                if after_first:
                    after_first(p)
                with eng.Fori(p * NT + 1, (p + 1) * NT - p) as n:
                    emit(n)
            emit(2 * NT - 1, more=False)

        def score_head(it, s):
            return (it + 1, s + LEAD) if s < H - LEAD else (it + 2, s + LEAD - H)

        def guests(it, s):
            counts = [it + (s > 1), it + (s > 3), it + 3 + (s > 5), it - 1 + (s > 6)]
            if isinstance(it, int):
                return sum(min(max(n, 0), NB) for n in counts)
            return it * 4 + (2 + (s > 1) + (s > 3) + (s > 5) + (s > 6))

        def settled(eng):
            eng.sem_inc(passed, 1)

        block = outer.enter_context(nc.Block())

        @block.sync
        def _(sp):
            sp.dma_start(weighted[:, :], w_router[0].partition_broadcast(P)).then_inc(wr_loaded, 16)
            sp.dma_start(wdiff[:, :], w_router[1].partition_broadcast(P)).then_inc(wr_loaded, 16)

            def load_inputs(b):
                wait(sp, krest_done, b)
                wait(sp, k1_done, b)
                wait(sp, v_t, b)
                sp.dma_start(c_in[:, :], ctx_dh[b]).then_inc(c_loaded, 16)
                wait(sp, q_done, b)
                sp.dma_start(x_in[:, :], x_dh[b]).then_inc(x_loaded, 16)

            load_inputs(0)
            for kind, block_of in ((0, wfc_block), (1, wpr_block)):
                sp.dma_start(wst[kind][:, :], block_of(0)).then_inc(wst_loaded[kind], 16)

            def step(it):
                if has(it + 2):
                    b = it + 2
                    wait(sp, shifted, (b - RING + 1) * NQ * GH)
                    settled(sp)
                    wait(sp, k3_done, b + 1)
                    for n, part in enumerate(K_PART):
                        if part == 0:
                            wait(sp, k1_done, b + 1)
                        if part == 1:
                            wait(sp, k2_done, b + 1)
                        sp.dma_start(kst[n * DH:(n + 1) * DH, b % RING, :, :],
                                     kparts[:, part, :]).then_inc(k_stacked, 16)
                if has(it - 1):
                    wait(sp, mid_done, it - 1)
                    sp.dma_start(x_res[:, :], x[it - 1]).then_inc(res_loaded, 16)
                if has(it + 2):
                    wait(sp, q1_done, b + 1)
                    wait(sp, q2_done, b + 1)
                    wait(sp, q3_done, b + 1)
                    settled(sp)
                    for n, part in enumerate(Q_PART):
                        sp.dma_start(qst[n * DH:(n + 1) * DH, b % RING, :, :],
                                     qparts[:, part, :]).then_inc(q_stacked, 16)
                if has(it):
                    store_weights(it, 0)
                if has(it + 1):
                    b = it + 1
                    for n, made in ((0, c1_done), (1, c2_done)):
                        sp.wait_ge(made, b + 1)
                        sp.dma_start(qst[KR + n:KR + n + 1, b % RING, :, :],
                                     cparts[:, n, :]).then_inc(c_stacked, 16)
                if has(it):
                    store_weights(it, 1)
                if has(it + 4):
                    load_inputs(it + 4)

            def store_weights(it, w):
                if w == 0:
                    def dst(part):
                        return up_t[it // 16, :, (it // 8) % 2, part, :, bass.ds(it % 8 * P, P)]
                else:
                    def dst(part):
                        return down_t[(it % 4) // 2, :, it // 16, part, bass.ds((it % 2) * 4, 4),
                                      bass.ds((it // 4) % 4 * P, P)]
                sp.wait_ge(w_split[w], it + 1)
                settled(sp)
                sp.dma_start(dst(HI), w_hi[w][:, :, :].bitcast(F32)).then_inc(w_stored[w], 16)
                sp.dma_start(dst(LO), w_lo[w][:, :, :].bitcast(F32)).then_inc(w_stored[w], 16)
                if has(it + 1):
                    block_of = (wfc_block, wpr_block)[w]
                    sp.dma_start(wst[w][:, :], block_of(it + 1)).then_inc(wst_loaded[w], 16)

            iterations(sp, step)

            def load_up(p):
                for e in range(NE):
                    for part in (HI, LO):
                        sp.dma_start(up_sb[:, e, part, :, :].bitcast(F32), up_t[p, :, e, part, :, :]).then_inc(up_loaded[e], 16)

            def load_down(p):
                for e in range(NE):
                    for part in (HI, LO):
                        sp.dma_start(down_sb[:, e, part, :, :].bitcast(F32),
                                     down_t[p, :, e, part, :, :]).then_inc(down_loaded[e], 16)

            sp.wait_ge(w_stored[0], 32 * NB)
            load_up(0)
            sp.wait_ge(scalar_left, 1)
            sp.wait_ge(vector_left, 1)
            sp.wait_ge(scattered, 16 * NB)
            sp.wait_ge(padded, 16)

            def load_rows(n):
                if not isinstance(n, int) or n >= 3:
                    sp.wait_ge(y_done, n - 2)
                    settled(sp)
                wait(sp, rows_loaded, 16 * n)
                if not isinstance(n, int):
                    settled(sp)
                sp.dma_start(rows_in[:, n % 3, :],
                             sorted_rows[bass.ds(n % NT * P, P), :]).then_inc(rows_loaded, 16)

            def store_part(n):
                sp.wait_ge(y_done, n + 1)
                settled(sp)
                sp.dma_start(partial[bass.ds(n * P, P), :], y_out[:, :]).then_inc(part_stored, 16)

            def load_part(n):
                sp.wait_ge(part_loaded, 16 * (n - NT)) if not isinstance(n, int) or n > NT else None
                if not isinstance(n, int):
                    settled(sp)
                sp.dma_start(part_in[:, n % 3, :],
                             partial[bass.ds((n - NT) * P, P), :]).then_inc(part_loaded, 16)

            load_rows(0)
            sp.wait_ge(w_stored[1], 32 * NB)
            load_down(0)
            load_rows(1)
            load_rows(2)
            with sp.Fori(3, NT + 2) as n:
                load_rows(n)
                store_part(n - 3)
            sp.wait_ge(h_done, HS * NT)
            load_up(1)
            sp.wait_ge(y_psum, HS * NT)
            load_down(1)
            store_part(NT - 1)
            sp.wait_ge(part_stored, 16 * NT)
            load_part(NT)
            load_part(NT + 1)
            with sp.Fori(NT + 2, 2 * NT) as n:
                load_rows(n)
                load_part(n)

        @block.gpsimd
        def _(pool):
            pool.memset(ident[:, :], 0.0).then_inc(const_a, 1)
            pool.memset(upper[:, :], 1.0).then_inc(const_a, 1)
            pool.memset(ones[:, :], 1.0).then_inc(const_ready, 1)
            pool.memset(neghalf[:, :], -0.5).then_inc(const_ready, 1)
            pool.wait_ge(const_a, 2)
            pool.affine_select(out=ident[:, :], in_=ident[:, :], compare_op=ALU.not_equal, fill=1.0, base=0,
                               pattern=[[-1, P]], channel_multiplier=1).then_inc(const_ready, 1)
            pool.affine_select(out=upper[:, :], in_=upper[:, :], compare_op=ALU.is_gt, fill=0.0, base=0,
                               pattern=[[1, P]], channel_multiplier=-1).then_inc(const_ready, 1)
            pool.iota(ident_i[:, :], pattern=[[0, 1]], base=0, channel_multiplier=1).then_inc(const_ready, 1)
            pool.iota(starts_i[:, :], pattern=[[P, NT]], base=0, channel_multiplier=0).then_inc(const_ready, 1)
            pool.wait_ge(const_ready, 6)

            def power(dst, var, tmp, have, mid, done, b):
                pool.wait_ge(have, b + 1)
                settled(pool)
                pool.tensor_scalar(tmp[:, :], var, EPS, None, ALU.add).then_inc(mid, 1)
                pool.wait_ge(mid, b + 1)
                pool.tensor_tensor(dst, tmp[:, :], neghalf[:, :], ALU.pow).then_inc(done, 1)

            def values(b, g):
                wait(pool, pv_done, NQ * (b - 1) + NCH * (g + 1))
                pool.wait_ge(guest_read, guests(b - 3, 6))
                pool.tensor_copy(vt[:, g * GH:(g + 1) * GH, :, 0:DH],
                                 vt_next[:, b % RING, g * GH:(g + 1) * GH, :, :]).then_inc(v_half[g], 1)

            def split_weights(it, w):
                pool.wait_ge(w_rounded[w], it + 1)
                wait(pool, w_stored[w], 32 * it)
                pool.tensor_tensor(w_lo[w][:, :, :], w_raw[w][:, :, :], w_hi[w][:, :, :].bitcast(F32),
                                   ALU.subtract).then_inc(w_split[w], 1)

            def step(it):
                b = it + 3
                if has(it):
                    values(it, 1)
                if has(b):
                    pool.wait_ge(k1_done, b + 1)
                    wait(pool, k2_done, b)
                    pool.tensor_tensor(krest[:, :], c_in[:, :], kparts[:, 0, :], ALU.subtract).then_inc(krest_done, 1)
                    power(rstd1[:, :], mv1[:, 1:2], ve1, mv1_done, ve1_done, rstd1_done, b)
                if has(it - 1):
                    power(row[:, M + 1:M + 2], row[:, M + 1:M + 2], ve2, mv2_done, ve2_done, rstd2_done, it - 1)
                if has(it):
                    split_weights(it, 0)
                if has(b):
                    pool.wait_ge(k2_done, b + 1)
                    pool.wait_ge(krest_done, b + 1)
                    pool.tensor_tensor(kparts[:, 2, :], krest[:, :], kparts[:, 1, :], ALU.subtract).then_inc(k3_done, 1)
                if has(it + 1):
                    values(it + 1, 0)
                if has(it):
                    split_weights(it, 1)
                if has(b):
                    pool.wait_ge(q1_done, b + 1)
                    wait(pool, q2_done, b)
                    pool.tensor_tensor(qrest[:, :], qf[:, :], qparts[:, 0, :], ALU.subtract).then_inc(qrest_done, 1)
                    pool.wait_ge(q2_done, b + 1)
                    pool.wait_ge(qrest_done, b + 1)
                    pool.tensor_tensor(qparts[:, 2, :], qrest[:, :], qparts[:, 1, :], ALU.subtract).then_inc(q3_done, 1)
                if has(it - 1):
                    pool.wait_ge(slot_done, it)
                    pool.wait_ge(row_done, it)
                    settled(pool)
                    pool.indirect_dma_start(
                        out=sorted_rows[:, :], out_offset=bass.IndirectOffsetOnAxis(ap=slot[:, 0:1], axis=0),
                        in_=row[:, :], in_offset=None).then_inc(scattered, 16)

            iterations(pool, step)
            pool.wait_ge(pad_done, 1)
            pool.indirect_dma_start(
                out=sorted_rows[:, :], out_offset=bass.IndirectOffsetOnAxis(ap=pad_slot[:, 0:1], axis=0),
                in_=pad_row[:, :], in_offset=None).then_inc(padded, 16)

            with pool.Fori(NT, 2 * NT) as n:
                pool.wait_ge(y_done, n + 1)
                settled(pool)
                pool.indirect_dma_start(
                    out=out[:, :], out_offset=bass.IndirectOffsetOnAxis(ap=y_token[:, 0:1], axis=0),
                    in_=y_out[:, :], in_offset=None, bounds_check=NTOK - 1, oob_is_err=False).then_inc(y_stored, 16)
            pool.wait_ge(y_stored, 16 * NT)

        @block.scalar
        def _(sc):
            def exps(b, q):
                for hh in range(GH):
                    n = (b * NQ + q) * GH + hh
                    sc.wait_ge(shifted, n + 1)
                    if hh == 0:
                        wait(sc, pv_done, b * NQ + q - 3)
                    nc.scalar.activation(probs[:, q % 4, hh, :], st_bank[hh % 2][:, :], ACT.Exp,
                                         scale=SCALE).then_inc(exped, 1)

            def step(it):
                b = it + 3
                for s in range(NQ):
                    if s == 0 and has(it - 1):
                        o_evac(it - 1, 1)
                    if s == 4 and has(it):
                        o_evac(it, 0)
                    if s < NQ - 1 and has(it):
                        exps(it, s + 1)
                    if s == NQ - 1 and has(it + 1):
                        exps(it + 1, 0)
                    if s == 1 and has(it):
                        take_weights(it, 0)
                    if s == 2 and has(b):
                        sc.wait_ge(c_loaded, 16 * (b + 1))
                        wait(sc, k_stacked, 16 * SPLIT * b)
                        nc.scalar.activation(kparts[:, 0, :], c_in[:, :], ACT.Copy).then_inc(k1_done, 1)
                    if s == 3 and has(it):
                        take_weights(it, 1)
                    if (s == 2 or s == 4) and has(it):
                        round_weights(it, (s - 2) // 2)
                    if s == 4 and has(b):
                        sc.wait_ge(krest_done, b + 1)
                        nc.scalar.activation(kparts[:, 1, :], krest[:, :], ACT.Copy).then_inc(k2_done, 1)
                    if s == 5 and has(b):
                        sc.wait_ge(v_t, b + 1)
                        wait(sc, v_half[1], b - RING + 1)
                        nc.scalar.activation(
                            vt_next[:, b % RING, :, :, :].rearrange("p h c d -> p c h d"),
                            st_bank[0][:, :].rearrange("p (c d h) -> p c h d", c=NCH, h=H),
                            ACT.Copy).then_inc(guest_read, 1)
                    if s == 5 and has(b):
                        sc.wait_ge(q_done, b + 1)
                        wait(sc, q_stacked, 16 * SPLIT * b)
                        nc.scalar.activation(qparts[:, 0, :], qf[:, :], ACT.Copy).then_inc(q1_done, 1)
                    if s == 6 and has(it - 1):
                        sc.wait_ge(ranked, it)
                        wait(sc, count_done, it - 1)
                        nc.scalar.activation(ranks[:, :], st_bank[0][:, 0:2], ACT.Copy).then_inc(guest_read, 1)
                    if s == 7 and has(b):
                        sc.wait_ge(qrest_done, b + 1)
                        nc.scalar.activation(qparts[:, 1, :], qrest[:, :], ACT.Copy).then_inc(q2_done, 1)

            def take_weights(it, w):
                sc.wait_ge(w_t[w], it + 1)
                wait(sc, w_split[w], it)
                nc.scalar.activation(w_raw[w][:, :, :], st_bank[0][:, :].rearrange("p (k n) -> p k n", k=NCH),
                                     ACT.Copy).then_inc(guest_read, 1)

            def round_weights(it, w):
                sc.wait_ge(guest_read, guests(it, 2 + 2 * w))
                wait(sc, w_stored[w], 32 * it)
                nc.scalar.activation(w_hi[w][:, :, :], w_raw[w][:, :, :], ACT.Copy).then_inc(w_rounded[w], 1)

            def o_evac(b, g):
                sc.wait_ge(pv_done, NQ * b + NCH * (g + 1))
                wait(sc, o_t[g], b)
                nc.scalar.activation(o_sb[:, g, :], o_bank[:, :], ACT.Copy).then_inc(o_moved[g], 1)

            iterations(sc, step)
            nc.scalar.activation(left_mark[:, :], neghalf[:, :], ACT.Copy).then_inc(scalar_left, 1)
            sc.wait_ge(vector_left, 1)

            def round_rows(n):
                sc.wait_ge(f_t, n + 1)
                wait(sc, h_done, HS * n)
                nc.scalar.activation(f_lnt[:, HI, :, :], xt_bank[:, :].rearrange("p (k n) -> p k n", k=KC),
                                     ACT.Copy).then_inc(f_hi_done, 1)

            def tile(n, more=True):
                sc.wait_ge(absd_done, n + 1)
                wait(sc, den_done, n)
                nc.scalar.activation(expd[:, :], absd[:, :], ACT.Exp, scale=-1.0).then_inc(expd_done, 1)

                def turned(hs):
                    m = n * HS + hs
                    sc.wait_ge(a_t, m + 1)
                    wait(sc, y_psum, m - 1)
                    nc.scalar.activation(act_t[:, HI, 4 * hs:4 * hs + 4, :],
                                         at_bank[hs % 2][:, :].rearrange("p (k n) -> p k n", k=4),
                                         ACT.Copy).then_inc(a_hi_done, 1)

                def slice_(hs):
                    m = n * HS + hs
                    sc.wait_ge(h_done, m + 1)
                    nc.scalar.activation(half_h[:, hs % 2, :], h_bank[hs % 2], ACT.Copy,
                                         scale=0.5).then_inc(half_done, 1)
                    sc.wait_ge(leaky_done, m + 1)
                    wait(sc, a_t, m - 1)
                    nc.scalar.activation(act[:, hs % 2, :], leaky[:, hs % 2, :], ACT.Square).then_inc(act_done, 1)

                slice_(0)
                turned(0)
                slice_(1)
                if more:
                    round_rows(n + 1)
                turned(1)

            round_rows(0)
            tiles(sc, tile)

        @block.tensor
        def _(pe):
            pe.wait_ge(const_ready, 6)
            pe.wait_ge(v_const, 2)

            def transposed(b, src, dst, done):
                for k in range(NCH):
                    last = nc.tensor.transpose(dst[:, k * P:(k + 1) * P], src[:, k * P:(k + 1) * P], ident[:, :])
                last.then_inc(done, 1)

            def score(b, h, j):
                n = (b * H + h) * 2 + j // 2
                if h == 0 and j == 0:
                    pe.wait_ge(k_stacked, 16 * SPLIT * (b + 1))
                    pe.wait_ge(q_stacked, 16 * SPLIT * (b + 1))
                if j % 2 == 0:
                    wait(pe, maxed, n - 1)
                last = nc.tensor.matmul(s_pair[j // 2][:, j % 2, :], qst[0:KR, b % RING, h, j * P:(j + 1) * P],
                                        kst[0:KR, b % RING, h, :], start=True, stop=True)
                if j % 2 == 1:
                    last.then_inc(scored, 1)

            def shift(it, s, b, q, hh):
                n = (b * NQ + q) * GH + hh
                h, c = (q // NCH) * GH + hh, q % NCH
                if q == 0 and hh == 0:
                    pe.wait_ge(c_stacked, 32 * (b + 1))
                wait(pe, exped, n - 1)
                if hh == 0:
                    wait(pe, guest_read, guests(it, s))
                nc.tensor.matmul(st_bank[hh % 2][:, :], kst[0:KR + 2, b % RING, h, c * P:(c + 1) * P],
                                 qst[0:KR + 2, b % RING, h, :], start=True, stop=True).then_inc(shifted, 1)

            def product(b, q):
                g, c = q // NCH, q % NCH
                pe.wait_ge(exped, (b * NQ + q + 1) * GH)
                if c == 0:
                    pe.wait_ge(v_half[g], b + 1)
                    if g == 0:
                        wait(pe, o_moved[1], b)
                    else:
                        pe.wait_ge(o_moved[0], b + 1)
                for hh in range(GH):
                    last = nc.tensor.matmul(o_bank[32 * hh:32 * hh + 32, :], vt[:, g * GH + hh, c, :],
                                            probs[:, q % 4, hh, :], start=(c == 0), stop=(c == NCH - 1))
                last.then_inc(pv_done, 1)

            def guest(it, s):
                if (s == 1 or s == 3) and has(it):
                    w = s // 2
                    pe.wait_ge(wst_loaded[w], 16 * (it + 1))
                    bank_clear(it, s)
                    transposed(it, wst[w], st_bank[0], w_t[w])
                if s == 5 and has(it + 3):
                    pe.wait_ge(c_loaded, 16 * (it + 4))
                    bank_clear(it, s)
                    transposed(it + 3, c_in, st_bank[0], v_t)
                if s == 6 and has(it - 1):
                    pe.wait_ge(one_done, it)
                    bank_clear(it, s)
                    nc.tensor.matmul(st_bank[0][:, 0:1], upper[:, :], to_one[:, :], start=True, stop=True)
                    nc.tensor.matmul(st_bank[0][:, 1:2], ones[:, :], to_one[:, :], start=True,
                                     stop=True).then_inc(ranked, 1)

            def bank_clear(it, s):
                n = (it * NQ + s + 1) * GH
                wait(pe, exped, made_tiles(n + 3))
                wait(pe, guest_read, guests(it, s))

            def made_tiles(n):
                return min(n, NB * NQ * GH) if isinstance(n, int) else n

            def made(n):
                return min(n, NB) if isinstance(n, int) else n

            def step(it):
                for s in range(NQ):
                    sb_, sh = score_head(it, s)
                    tb, tq = (it, s + 1) if s < NQ - 1 else (it + 1, 0)
                    for j in range(NCH):
                        if has(tb):
                            shift(it, s, tb, tq, j)
                        if has(sb_):
                            score(sb_, sh, j)
                    guest(it, s)
                    if has(it):
                        product(it, s)
                    if s == 0 and has(it - 1):
                        pe.wait_ge(o_moved[1], it)
                        pe.wait_ge(o_normed[0], it)
                        transposed(it - 1, o_sb[:, 1, :], m_bank, o_t[1])
                    if s == 2 and has(it - 1):
                        pe.wait_ge(o_normed[1], it)
                        for k in range(NCH):
                            last = nc.tensor.transpose(m_bank[:, k * P:(k + 1) * P], o_norm[:, k, :], ident[:, :])
                        last.then_inc(o_back, 1)
                    if s == 4 and has(it + 1):
                        pe.wait_ge(maxed, (it + 2) * H * 2)
                        pe.wait_ge(head_copied, it + 2)
                        wait(pe, mid_done, it)
                        nc.tensor.transpose(m_bank[0:H * NCH, 0:P], maxes[:, :], ident[:, :]).then_inc(max_t, 1)
                    if s == 6 and has(it):
                        pe.wait_ge(o_moved[0], it + 1)
                        wait(pe, crest_done, made(it + 2))
                        wait(pe, mid_done, it)
                        transposed(it, o_sb[:, 0, :], m_bank, o_t[0])

            iterations(pe, step)

            pe.wait_ge(scalar_left, 1)
            pe.wait_ge(vector_left, 1)
            pe.wait_ge(table_done, 1)

            def flip(n):
                pe.wait_ge(f_ln_done, n + 1)
                wait(pe, f_t_moved, n)
                transposed(n, f_ln, xt_bank, f_t)

            PRODUCTS = ((HI, HI), (LO, HI), (HI, LO))

            def tile(n, more=True):
                expert = pe.value_load(expert_of[0:1, bass.ds(n % NT, 1)], min_val=0, max_val=NE - 1)

                def up(hs):
                    m = n * HS + hs
                    wait(pe, leaky_done, m - 1)
                    for k in range(KC):
                        for a, w in PRODUCTS:
                            last = nc.tensor.matmul(h_bank[hs % 2], f_lnt[:, a, k, :],
                                                    up_sb[:, expert, w, k, hs * 512:(hs + 1) * 512],
                                                    start=(k == 0 and (a, w) == PRODUCTS[0]),
                                                    stop=(k == KC - 1 and (a, w) == PRODUCTS[-1]))
                    last.then_inc(h_done, 1)

                pe.wait_ge(f_t_moved, n + 1)
                if isinstance(n, int) and n % NT == 0:
                    pe.wait_ge(up_loaded[0], 32 * (n // NT + 1))
                up(0)
                before = expert_before(n)
                down(n - 1, before, 0)
                turn(n, 0)
                up(1)
                if more:
                    flip(n + 1)
                down(n - 1, before, 1)
                turn(n, 1)

            def expert_before(n):
                if isinstance(n, int) and n == 0:
                    return None
                return pe.value_load(expert_of[0:1, bass.ds((n + NT - 1) % NT, 1)], min_val=0, max_val=NE - 1)

            def turn(n, hs):
                m = n * HS + hs
                pe.wait_ge(act_done, m + 1)
                wait(pe, a_t_moved, m - 1)
                transposed(n, act[:, hs % 2, :], at_bank[hs % 2], a_t)

            def down(n, expert, hs):
                if isinstance(n, int) and n < 0:
                    return
                if isinstance(n, int) and n % NT == 0 and hs == 0:
                    pe.wait_ge(down_loaded[0], 32 * (n // NT + 1))
                pe.wait_ge(a_t_moved, n * HS + hs + 1)
                if hs == 0:
                    wait(pe, y_done, n)
                for k in range(4 * hs, 4 * hs + 4):
                    for a, w in PRODUCTS:
                        last = nc.tensor.matmul(y_bank[:, :], act_t[:, a, k, :], down_sb[:, expert, w, k, :],
                                                start=(k == 0 and (a, w) == PRODUCTS[0]),
                                                stop=(k == HC - 1 and (a, w) == PRODUCTS[-1]))
                last.then_inc(y_psum, 1)

            flip(0)
            for p in range(2):
                tile(p * NT)
                pe.wait_ge(up_loaded[1], 32 * (p + 1))
                tile(p * NT + 1)
                pe.wait_ge(down_loaded[1], 32 * (p + 1))
                with pe.Fori(p * NT + 2, (p + 1) * NT - p) as n:
                    tile(n)
            tile(2 * NT - 1, more=False)
            before = expert_before(2 * NT)
            down(2 * NT - 1, before, 0)
            down(2 * NT - 1, before, 1)

        @block.vector
        def _(dve):
            nc.vector.memset(kst[KR:KR + 2, :, :, :], 1.0).then_inc(v_const, 1)
            nc.vector.memset(vt[:, :, :, DH:2 * DH], 1.0).then_inc(v_const, 1)
            nc.vector.memset(count1[:, :], 0.0).then_inc(count_init, 1)
            nc.vector.memset(pad_row[:, :], 0.0).then_inc(pad_a, 1)
            dve.wait_ge(const_ready, 6)
            nc.vector.tensor_copy(token[:, :], ident_i[:, :]).then_inc(count_init, 1)
            nc.vector.tensor_copy(starts[:, :], starts_i[:, :]).then_inc(table_a, 1)
            dve.wait_ge(wr_loaded, 32)
            nc.vector.tensor_tensor(wdiff[:, :], wdiff[:, :], weighted[:, :], ALU.subtract).then_inc(wdiff_ready, 1)
            dve.wait_ge(count_init, 2)
            dve.wait_ge(wdiff_ready, 1)

            def norm(b, g):
                dve.wait_ge(o_t[g], b + 1)
                got = m_bank[:, :].rearrange("p (j h r) -> p j h r", j=NCH, h=GH)
                nc.vector.reciprocal(rsum[:, :, :], got[:, :, :, DH]).then_inc(rsum_done[g], 1)
                dve.wait_ge(rsum_done[g], b + 1)
                nc.vector.tensor_tensor(
                    o_norm[:, :, g * GH * DH:(g + 1) * GH * DH].rearrange("p j (h r) -> p j h r", h=GH),
                    got[:, :, :, 0:DH], rsum[:, :, :].unsqueeze(3).to_broadcast([P, NCH, GH, DH]),
                    ALU.mult).then_inc(o_normed[g], 1)

            def maxima(b, h, pair):
                dst = max_head if h < LEAD else maxes
                dve.wait_ge(scored, (b * H + h) * 2 + pair + 1)
                nc.vector.reduce_max(dst[:, h * NCH + 2 * pair:h * NCH + 2 * pair + 2], s_pair[pair][:, :, :],
                                     AX.X).then_inc(maxed, 1)

            def step(it):
                b = it + 3
                for s in range(NQ):
                    if s == 0 and has(it + 1):
                        wait(dve, max_t, it + 1)
                        dve.wait_ge(maxed, (it + 1) * H * 2 + LEAD * 2)
                        nc.vector.tensor_copy(maxes[:, 0:LEAD * NCH], max_head[:, :]).then_inc(head_copied, 1)
                        dve.wait_ge(head_copied, it + 2)
                    sb_, sh = score_head(it, s)
                    if has(sb_):
                        maxima(sb_, sh, 0)
                    if s == 1 and has(it - 1):
                        norm(it - 1, 1)
                    if s == 2 and has(b):
                        dve.wait_ge(x_loaded, 16 * (b + 1))
                        nc.vector.bn_stats(stats1[:, :], x_in[:, :]).then_inc(stats1_done, 1)
                        dve.wait_ge(stats1_done, b + 1)
                        wait(dve, ve1_done, b)
                        settled(dve)
                        nc.vector.bn_aggr(mv1[:, :], stats1[:, :]).then_inc(mv1_done, 1)
                    if s == 3 and has(it - 1):
                        middle(it - 1)
                    if s == 4 and has(b):
                        dve.wait_ge(rstd1_done, b + 1)
                        wait(dve, q1_done, b)
                        wait(dve, qrest_done, b)
                        nc.vector.tensor_scalar(qf[:, :], x_in[:, :], mv1[:, 0:1], rstd1[:, 0:1], ALU.subtract,
                                                ALU.mult).then_inc(q_done, 1)
                    if s == 5 and has(it + 1):
                        shifts(it + 1)
                    if s == 7 and has(it):
                        norm(it, 0)
                    if has(sb_):
                        maxima(sb_, sh, 1)
                    if s == 4 and has(it - 1):
                        route(it - 1)
                    if s == 7 and has(it - 1):
                        place(it - 1)

            def middle(b):
                dve.wait_ge(o_back, b + 1)
                dve.wait_ge(res_loaded, 16 * (b + 1))
                wait(dve, scattered, 16 * b)
                nc.vector.tensor_tensor(row[:, 0:M], m_bank[:, :], x_res[:, :], ALU.add).then_inc(mid_done, 1)
                dve.wait_ge(mid_done, b + 1)
                nc.vector.bn_stats(stats2[:, :], row[:, 0:M]).then_inc(stats2_done, 1)
                dve.wait_ge(stats2_done, b + 1)
                settled(dve)
                nc.vector.bn_aggr(row[:, M:M + 2], stats2[:, :]).then_inc(mv2_done, 1)

            def route(b):
                dve.wait_ge(mv2_done, b + 1)
                nc.vector.scalar_tensor_tensor(out=weighted[:, :], in0=row[:, 0:M], scalar=row[:, M:M + 1], in1=wdiff[:, :],
                                               op0=ALU.subtract, op1=ALU.mult,
                                               accum_out=row[:, M + 2:M + 3]).then_inc(ldiff_done, 1)
                dve.wait_ge(ldiff_done, b + 1)
                wait(dve, ranked, b)
                nc.vector.tensor_scalar(to_one[:, :], row[:, M + 2:M + 3], 0.0, None, ALU.is_gt).then_inc(one_done, 1)

            def shifts(b):
                dve.wait_ge(max_t, b + 1)
                wait(dve, c_stacked, 32 * b)
                top = m_bank[0:H * NCH, 0:P]
                nc.vector.tensor_scalar(cparts[:, 0, :], top, -1.0, None, ALU.mult).then_inc(c1_done, 1)
                dve.wait_ge(c1_done, b + 1)
                nc.vector.scalar_tensor_tensor(out=crest[:, :], in0=top, scalar=-1.0, in1=cparts[:, 0, :],
                                               op0=ALU.mult, op1=ALU.subtract).then_inc(crest_done, 1)
                dve.wait_ge(crest_done, b + 1)
                nc.vector.tensor_copy(cparts[:, 1, :], crest[:, :]).then_inc(c2_done, 1)

            def place(b):
                dve.wait_ge(guest_read, guests(b + 1, 7))
                wait(dve, token_done, b)
                wait(dve, count_done, b)
                nc.vector.scalar_tensor_tensor(out=neg_a[:, :], in0=ranks[:, 0:1], scalar=count1[:, 0:1],
                                               in1=token[:, :], op0=ALU.add, op1=ALU.subtract).then_inc(nega_done, 1)
                nc.vector.scalar_tensor_tensor(out=neg_b[:, :], in0=token[:, :], scalar=float(CAP - 1),
                                               in1=to_one[:, :], op0=ALU.subtract, op1=ALU.mult).then_inc(negb_done, 1)
                dve.wait_ge(nega_done, b + 1)
                dve.wait_ge(negb_done, b + 1)
                nc.vector.scalar_tensor_tensor(out=slot[:, :], in0=neg_a[:, :], scalar=-1.0, in1=neg_b[:, :],
                                               op0=ALU.mult, op1=ALU.subtract).then_inc(slot_done, 1)
                dve.wait_ge(rstd2_done, b + 1)
                nc.vector.tensor_tensor(row[:, M + 2:M + 3], row[:, M + 2:M + 3], row[:, M + 1:M + 2], ALU.mult)
                nc.vector.tensor_copy(row[:, M + 3:M + 4].bitcast(I32), token[:, :]).then_inc(row_done, 1)
                nc.vector.tensor_scalar(token[:, :], token[:, :], float(P), None, ALU.add).then_inc(token_done, 1)
                nc.vector.tensor_tensor(count1[:, :], count1[:, :], ranks[:, 1:2], ALU.add).then_inc(count_done, 1)

            iterations(dve, step)

            dve.wait_ge(pad_a, 1)
            dve.wait_ge(count_done, NB)
            nc.vector.memset(pad_row[:, M + 3:M + 4].bitcast(I32), NTOK).then_inc(pad_a, 1)
            nc.vector.tensor_scalar(pad_f[:, :], count1[:, :], -1.0, float(NTOK), ALU.mult, ALU.add).then_inc(pad_a, 1)
            dve.wait_ge(pad_a, 3)
            nc.vector.tensor_tensor(pad_slot[:, :], pad_f[:, :], ident_i[:, :], ALU.add).then_inc(pad_done, 1)
            dve.wait_ge(table_a, 1)
            nc.vector.tensor_scalar(expert_of[:, :], starts[:, :], pad_f[0:1, 0:1], None, ALU.is_gt).then_inc(table_done, 1)
            dve.wait_ge(padded, 16)
            nc.vector.tensor_copy(left_mark2[:, :], neghalf[:, :]).then_inc(vector_left, 1)
            dve.wait_ge(scalar_left, 1)

            def normalise(i):
                dve.wait_ge(rows_loaded, 16 * (i + 1))
                wait(dve, f_t, i)
                nc.vector.tensor_scalar(f_ln[:, :], rows_in[:, i % 3, 0:M], rows_in[:, i % 3, M:M + 1],
                                        rows_in[:, i % 3, M + 1:M + 2], ALU.subtract,
                                        ALU.mult).then_inc(f_ln_done, 1)
                wait(dve, absd_done, i)
                nc.vector.tensor_scalar(negd[:, :], rows_in[:, i % 3, M + 2:M + 3], -1.0, None,
                                        ALU.mult).then_inc(negd_done, 1)
                dve.wait_ge(negd_done, i + 1)
                wait(dve, expd_done, i)
                nc.vector.tensor_tensor(absd[:, :], rows_in[:, i % 3, M + 2:M + 3], negd[:, :],
                                        ALU.max).then_inc(absd_done, 1)

            def take(i):
                dve.wait_ge(f_t, i + 1)
                dve.wait_ge(f_hi_done, i + 1)
                nc.vector.tensor_tensor(f_lnt[:, LO, :, :], xt_bank[:, :].rearrange("p (k n) -> p k n", k=KC),
                                        f_lnt[:, HI, :, :].bitcast(F32), ALU.subtract).then_inc(f_t_moved, 1)

            def leak(i, hs):
                n = i * HS + hs
                dve.wait_ge(half_done, n + 1)
                wait(dve, act_done, n - 1)
                nc.vector.tensor_tensor(leaky[:, hs % 2, :], h_bank[hs % 2], half_h[:, hs % 2, :],
                                        ALU.max).then_inc(leaky_done, 1)

            def turned(i, hs):
                dve.wait_ge(a_hi_done, i * HS + hs + 1)
                nc.vector.tensor_tensor(act_t[:, LO, 4 * hs:4 * hs + 4, :],
                                        at_bank[hs % 2][:, :].rearrange("p (k n) -> p k n", k=4),
                                        act_t[:, HI, 4 * hs:4 * hs + 4, :].bitcast(F32),
                                        ALU.subtract).then_inc(a_t_moved, 1)

            def weigh(i):
                dve.wait_ge(expd_done, i + 1)
                nc.vector.tensor_scalar(den[:, :], expd[:, :], 1.0, None, ALU.add).then_inc(den_done, 1)
                dve.wait_ge(den_done, i + 1)
                nc.vector.reciprocal(top_w[:, :], den[:, :]).then_inc(top_done, 1)

            def sum_up(i, second):
                dve.wait_ge(y_psum, (i + 1) * HS)
                dve.wait_ge(top_done, i + 1)
                if not second or (isinstance(i, int) and i == NT):
                    wait(dve, part_stored, 16 * i)
                else:
                    dve.wait_ge(y_stored, 16 * (i - NT))
                so_far = rows_in[:, i % 3, 0:M]
                if second:
                    dve.wait_ge(part_loaded, 16 * (i - NT + 1))
                    so_far = part_in[:, i % 3, :]
                nc.vector.scalar_tensor_tensor(out=y_out[:, :], in0=y_bank[:, :], scalar=top_w[:, 0:1],
                                               in1=so_far, op0=ALU.mult, op1=ALU.add).then_inc(y_summed, 1)
                nc.vector.tensor_copy(y_token[:, :], rows_in[:, i % 3, M + 3:M + 4].bitcast(I32)).then_inc(y_done, 1)

            def tile(i, second_before, more=True):
                leak(i, 0)
                if more:
                    normalise(i + 1)
                turned(i, 0)
                leak(i, 1)
                if more:
                    take(i + 1)
                if not isinstance(i, int) or i > 0:
                    sum_up(i - 1, second_before)
                weigh(i)
                turned(i, 1)

            normalise(0)
            take(0)
            for p in range(2):
                tile(p * NT, False)
                tile(p * NT + 1, p == 1)
                with dve.Fori(p * NT + 2, (p + 1) * NT - p) as n:
                    tile(n, p == 1)
            tile(2 * NT - 1, True, more=False)
            sum_up(2 * NT - 1, True)


_INS = ["x", "ctx_2048", "L0_ffn_w_router", "L0_ffn_w_fc", "L0_ffn_w_proj"]


def kernel(**inputs):
    import concourse.bacc as bacc
    import numpy as np
    from concourse import mybir as _mybir
    from concourse.bass_utils import run_bass_kernel_spmd

    nc = bacc.Bacc("TRN2", target_bir_lowering=False, num_devices=1)
    arrays, args = {}, []
    for name in _INS:
        a = np.ascontiguousarray(inputs[name])
        arrays[f"in_{name}"] = a
        args.append(nc.dram_tensor(f"in_{name}", a.shape, _mybir.dt.from_np(a.dtype), kind="ExternalInput").ap())
    batches, rows, feats = inputs["x"].shape
    out = nc.dram_tensor("out", (batches * rows, feats), _mybir.dt.float32, kind="ExternalOutput").ap()
    build_program(nc, *args, out)
    r = run_bass_kernel_spmd(nc, [arrays], core_ids=[0])
    return r.results[0]["out"].reshape(batches, rows, feats)
```

```python
from contextlib import ExitStack

import concourse.bass as bass
from concourse import mybir

ALU = mybir.AluOpType
ACT = mybir.ActivationFunctionType
AX = mybir.AxisListType
F32 = mybir.dt.float32
BF16 = mybir.dt.bfloat16
I32 = mybir.dt.int32
F32R = mybir.dt.float32r

P = 128


def wait(eng, sem, value):
    if not isinstance(value, int) or value > 0:
        eng.wait_ge(sem, value)


def build_program(nc, x, ctx, w_router, w_fc, w_proj, out):
    NB, D, M = x.shape
    H = 8
    DH = D // H
    NCH = M // P
    GH = 4
    NG = H // GH
    NQ = NG * NCH
    NE, HID, _ = w_fc.shape
    NTOK = NB * D
    CAP = NTOK + P
    NT = CAP // P
    KC = M // P
    HH = HID // 2
    HS = HH // 512
    HC = HH // P
    HI, LO = 0, 1
    ROW = M + 4
    LEAD = 4
    SPLIT = 6
    KR = SPLIT * DH
    EPS = 1e-5
    SCALE = 1.0 / float(DH) ** 0.5
    RING = 3
    K_PART = [0, 1, 0, 1, 2, 0]
    Q_PART = [0, 0, 1, 1, 0, 2]
    assert D == P and M == 512 and NQ == H and NB == NE * HID // P

    sorted_rows = nc.dram_tensor("sorted_rows", (CAP, ROW), F32, kind="Internal").ap()
    partial = nc.dram_tensor("partial", (CAP, M), F32, kind="Internal").ap()
    up_t = nc.dram_tensor("up_t", (2, P, NE, 2, KC, HH), F32, kind="Internal").ap()
    down_t = nc.dram_tensor("down_t", (2, P, NE, 2, HC, M), F32, kind="Internal").ap()
    x_dh = x.rearrange("b (h d) m -> b d h m", d=DH)
    ctx_dh = ctx.rearrange("b (h d) m -> b d h m", d=DH)
    wfc_rows = w_fc.rearrange("e (r p) d -> (e r) p d", p=P)
    wpr_rows = w_proj.rearrange("e (r p) n -> (e r) p n", p=P)

    def wfc_block(n):
        return wfc_rows[(n // 8) % 2 * (HID // P) + n // 16 * HC + n % 8]

    def wpr_block(n):
        return wpr_rows[n // 4, :, bass.ds((n % 4) * 512, 512)]

    with ExitStack() as outer:
        def sem(name):
            return outer.enter_context(nc.semaphore(name))

        def psum(name, shape):
            return outer.enter_context(nc.psum_tensor(name, shape, F32))

        def keep(name, shape, dt):
            return outer.enter_context(nc.sbuf_tensor(name, shape, dt))

        v_bank = [psum(f"v_bank{n}", [P, 512]) for n in range(4)]
        a_bank = [psum(f"a_bank{n}", [P, 512]) for n in range(3)]
        o_bank = psum("o_bank", [P, 512])

        ident = keep("ident", [P, P], F32)
        left_mark = keep("left_mark", [P, 1], F32)
        left_mark2 = keep("left_mark2", [P, 1], F32)
        neghalf = keep("neghalf", [P, 1], F32)
        expert_of = keep("expert_of", [1, NT], I32)
        up_sb = keep("up_sb", [P, NE, 2, KC, HH], F32R)

        inner = ExitStack()

        def sb(name, shape, dt):
            return inner.enter_context(nc.sbuf_tensor(name, shape, dt))

        kst = sb("kst", [P, RING, H, M], BF16)
        qst = sb("qst", [P, RING, H, M], BF16)
        probs = sb("probs", [P, 4, GH, M], F32)
        x_in = sb("x_in", [P, M], F32)
        c_in = sb("c_in", [P, M], F32)
        x_res = sb("x_res", [P, M], F32)
        kparts = sb("kparts", [P, 3, M], BF16)
        qparts = sb("qparts", [P, 3, M], BF16)
        krest = sb("krest", [P, M], F32)
        qrest = sb("qrest", [P, M], F32)
        qf = sb("qf", [P, M], F32)
        vt = sb("vt", [P, H, NCH, 2 * DH], F32)
        vt_next = sb("vt_next", [P, RING, H, NCH, DH], F32)
        max_head = sb("max_head", [P, LEAD * NCH], F32)
        maxes = sb("maxes", [P, H * NCH], F32)
        cparts = sb("cparts", [H * NCH, 2, P], BF16)
        crest = sb("crest", [H * NCH, P], F32)
        o_sb = sb("o_sb", [P, NG, M], F32)
        o_norm = sb("o_norm", [P, NCH, D], F32)
        rsum = sb("rsum", [P, NCH, GH], F32)
        row = sb("row", [P, ROW], F32)
        weighted = sb("weighted", [P, M], F32)
        wdiff = sb("wdiff", [P, M], F32)
        stats1 = sb("stats1", [P, 6], F32)
        mv1 = sb("mv1", [P, 2], F32)
        ve1 = sb("ve1", [P, 1], F32)
        rstd1 = sb("rstd1", [P, 1], F32)
        stats2 = sb("stats2", [P, 6], F32)
        ve2 = sb("ve2", [P, 1], F32)
        to_one = sb("to_one", [P, 1], BF16)
        upper = sb("upper", [P, P], BF16)
        ones = sb("ones", [P, P], BF16)
        count1 = sb("count1", [P, 1], F32)
        ident_i = sb("ident_i", [P, 1], I32)
        token = sb("token", [P, 1], F32)
        ahead, front, back, to_back, slot_f = (
            sb(n, [P, 1], F32) for n in ("ahead", "front", "back", "to_back", "slot_f"))
        ranks = sb("ranks", [P, 2], F32)
        slot = sb("slot", [P, 1], I32)
        pad_row = sb("pad_row", [P, ROW], F32)
        pad_slot = sb("pad_slot", [P, 1], I32)
        pad_f = sb("pad_f", [P, 1], F32)
        starts_i = sb("starts_i", [1, NT], I32)
        starts = sb("starts", [1, NT], F32)
        wst = [sb("wst0", [P, 512], F32), sb("wst1", [P, 512], F32)]
        w_raw = [sb("w_raw0", [P, NCH, P], F32), sb("w_raw1", [P, NCH, P], F32)]
        w_hi = [sb("w_hi0", [P, NCH, P], F32R), sb("w_hi1", [P, NCH, P], F32R)]
        w_lo = [sb("w_lo0", [P, NCH, P], F32R), sb("w_lo1", [P, NCH, P], F32R)]
        inner.close()

        second = outer.enter_context(ExitStack())

        def sb2(name, shape, dt):
            return second.enter_context(nc.sbuf_tensor(name, shape, dt))

        down_sb = sb2("down_sb", [P, 3, 2, HC, M], F32R)
        part_in = sb2("part_in", [P, 3, M], F32)
        rows_in = sb2("rows_in", [P, 3, ROW], F32)
        f_ln = sb2("f_ln", [P, M], F32)
        f_lnt = sb2("f_lnt", [P, 2, KC, P], F32R)
        half_h = sb2("half_h", [P, 2, 512], F32)
        leaky = sb2("leaky", [P, 2, 512], F32)
        act = sb2("act", [P, 2, 512], F32)
        act_t = sb2("act_t", [P, 2, HC, P], F32R)
        absd = sb2("absd", [P, 1], F32)
        negd = sb2("negd", [P, 1], F32)
        expd = sb2("expd", [P, 1], F32)
        den = sb2("den", [P, 1], F32)
        top_w = sb2("top_w", [P, 1], F32)
        y_out = sb2("y_out", [P, M], F32)
        y_token = sb2("y_token", [P, 1], I32)

        h_bank, xt_bank = v_bank[0:2], v_bank[2]
        at_bank, y_bank = a_bank[0:2], o_bank

        x_loaded, c_loaded, res_loaded = sem("x_loaded"), sem("c_loaded"), sem("res_loaded")
        wr_loaded = sem("wr_loaded")
        wst_loaded = [sem("wst_loaded0"), sem("wst_loaded1")]
        const_a, const_ready = sem("const_a"), sem("const_ready")
        v_const = sem("v_const")
        wdiff_ready = sem("wdiff_ready")
        k1_done, krest_done, k2_done, k3_done = (sem(n) for n in ("k1_done", "krest_done", "k2_done", "k3_done"))
        q1_done, qrest_done, q2_done, q3_done = (sem(n) for n in ("q1_done", "qrest_done", "q2_done", "q3_done"))
        stats1_done, mv1_done, ve1_done, rstd1_done, q_done = (
            sem(n) for n in ("stats1_done", "mv1_done", "ve1_done", "rstd1_done", "q_done"))
        k_stacked, q_stacked = sem("k_stacked"), sem("q_stacked")
        v_filled, v_read = sem("v_filled"), sem("v_read")
        a_filled, a_read = sem("a_filled"), sem("a_read")
        head_copied, c1_done, c2_done, c_stacked = (
            sem(n) for n in ("head_copied", "c1_done", "c2_done", "c_stacked"))
        pv_done, v_half = sem("pv_done"), [sem("v_half0"), sem("v_half1")]
        o_moved = [sem("o_moved0"), sem("o_moved1")]
        rsum_done = [sem("rsum_done0"), sem("rsum_done1")]
        stats2_done, mv2_done, ve2_done, rstd2_done = (
            sem(n) for n in ("stats2_done", "mv2_done", "ve2_done", "rstd2_done"))
        ldiff_done, one_done, front_done, back_done = (
            sem(n) for n in ("ldiff_done", "one_done", "front_done", "back_done"))
        slot_done, count_done, token_done, row_done, scattered = (
            sem(n) for n in ("slot_done", "count_done", "token_done", "row_done", "scattered"))
        pad_a, pad_done, table_a, table_done, padded = (
            sem(n) for n in ("pad_a", "pad_done", "table_a", "table_done", "padded"))
        w_rounded = [sem("w_rounded0"), sem("w_rounded1")]
        w_split = [sem("w_split0"), sem("w_split1")]
        w_stored = [sem("w_stored0"), sem("w_stored1")]
        up_loaded, up_slice_loaded = sem("up_loaded"), [sem("up_slice_loaded0"), sem("up_slice_loaded1")]
        down_loaded = [sem("down_loaded0"), sem("down_loaded1"), sem("down_loaded2")]
        rows_loaded, part_loaded, part_stored = sem("rows_loaded"), sem("part_loaded"), sem("part_stored")
        f_hi_done, a_hi_done = sem("f_hi_done"), sem("a_hi_done")
        f_ln_done, f_t, f_t_moved = sem("f_ln_done"), sem("f_t"), sem("f_t_moved")
        h_done, half_done, leaky_done, act_done, a_t, a_t_moved = (
            sem(n) for n in ("h_done", "half_done", "leaky_done", "act_done", "a_t", "a_t_moved"))
        negd_done, absd_done, expd_done, den_done, top_done = (
            sem(n) for n in ("negd_done", "absd_done", "expd_done", "den_done", "top_done"))
        y_psum, y_done, y_stored = sem("y_psum"), sem("y_done"), sem("y_stored")
        y_summed, count_init, passed = sem("y_summed"), sem("count_init"), sem("passed")
        scalar_left, vector_left = sem("scalar_left"), sem("vector_left")

        def has(b):
            return not isinstance(b, int) or 0 <= b < NB

        def iterations(eng, emit):
            for it in range(-3, 2):
                emit(it)
            with eng.Fori(2, NB - 4) as it:
                emit(it)
            for it in range(NB - 4, NB + 1):
                emit(it)

        def score_head(it, s):
            return (it + 1, s + LEAD) if s < H - LEAD else (it + 2, s + LEAD - H)

        MORE = NCH
        V_ORDER = [(s, j) for s in range(NQ) for j in range(NCH + (s in (0, 2, 4, 6)))]
        A_ORDER = [(s, j) for s in range(NQ) for j in range(GH + (s in (1, 3, 5, 6)))]

        def quad(it, s):
            return (it, s + 1) if s < NQ - 1 else (it + 1, 0)

        def v_exists(it, s, j):
            return has(score_head(it, s)[0]) if j < MORE else has(it + {0: -1, 2: -1, 4: 1, 6: 0}[s])

        def a_exists(it, s, j):
            return has(quad(it, s)[0]) if j < MORE else has(it + {1: 0, 3: 0, 5: 3, 6: -1}[s])

        def filled(order, exists, it, place):
            if not isinstance(it, int):
                return it * len(order) + (filled(order, exists, 2, place) - 2 * len(order))
            return sum(exists(t, *entry) for t in range(-3, NB + 1) for n, entry in enumerate(order)
                       if (t - it) * len(order) + n < place)

        def v_through(it, s, j):
            return filled(V_ORDER, v_exists, it, V_ORDER.index((s, j)) + 1)

        def a_through(it, s, j):
            return filled(A_ORDER, a_exists, it, A_ORDER.index((s, j)) + 1)

        def v_slot(it, s, j):
            n = V_ORDER.index((s, j))
            return v_bank[n % len(v_bank)], filled(V_ORDER, v_exists, it, n - len(v_bank) + 1)

        def a_slot(it, s, j):
            n = A_ORDER.index((s, j))
            return a_bank[n % len(a_bank)], filled(A_ORDER, a_exists, it, n - len(a_bank) + 1)

        def settled(eng):
            eng.sem_inc(passed, 1)

        block = outer.enter_context(nc.Block())

        @block.sync
        def _(sp):
            sp.sem_inc(up_loaded, 1)
            sp.sem_inc(down_loaded[1], 1)
            sp.dma_start(weighted[:, :], w_router[0].partition_broadcast(P)).then_inc(wr_loaded, 16)
            sp.dma_start(wdiff[:, :], w_router[1].partition_broadcast(P)).then_inc(wr_loaded, 16)

            def load_inputs(b):
                wait(sp, krest_done, b)
                wait(sp, k1_done, b)
                if not isinstance(b, int) or b > 0:
                    sp.wait_ge(a_read, a_through(b - 4, 5, MORE))
                sp.dma_start(c_in[:, :], ctx_dh[b]).then_inc(c_loaded, 16)
                wait(sp, q_done, b)
                sp.dma_start(x_in[:, :], x_dh[b]).then_inc(x_loaded, 16)

            load_inputs(0)
            for kind, block_of in ((0, wfc_block), (1, wpr_block)):
                sp.dma_start(wst[kind][:, :], block_of(0)).then_inc(wst_loaded[kind], 16)

            def step(it):
                if has(it + 2):
                    b = it + 2
                    if not isinstance(b, int) or b >= RING:
                        sp.wait_ge(a_filled, a_through(it - 1, 6, GH - 1))
                        settled(sp)
                    wait(sp, k3_done, b + 1)
                    for n, part in enumerate(K_PART):
                        if part == 0:
                            wait(sp, k1_done, b + 1)
                        if part == 1:
                            wait(sp, k2_done, b + 1)
                        sp.dma_start(kst[n * DH:(n + 1) * DH, b % RING, :, :],
                                     kparts[:, part, :]).then_inc(k_stacked, 16)
                if has(it - 1):
                    if not isinstance(it, int) or it > 1:
                        sp.wait_ge(v_read, v_through(it - 1, 2, MORE))
                    sp.dma_start(x_res[:, :], x[it - 1]).then_inc(res_loaded, 16)
                if has(it + 2):
                    wait(sp, q1_done, b + 1)
                    wait(sp, q2_done, b + 1)
                    wait(sp, q3_done, b + 1)
                    settled(sp)
                    for n, part in enumerate(Q_PART):
                        sp.dma_start(qst[n * DH:(n + 1) * DH, b % RING, :, :],
                                     qparts[:, part, :]).then_inc(q_stacked, 16)
                if has(it):
                    store_weights(it, 0)
                if has(it + 1):
                    b = it + 1
                    for n, made in ((0, c1_done), (1, c2_done)):
                        sp.wait_ge(made, b + 1)
                        sp.dma_start(qst[KR + n:KR + n + 1, b % RING, :, :],
                                     cparts[:, n, :]).then_inc(c_stacked, 16)
                if has(it):
                    store_weights(it, 1)
                if has(it + 4):
                    load_inputs(it + 4)
                if isinstance(it, int) and NB - 4 <= it < NB:
                    sp.wait_ge(w_stored[0], 32 * it)
                    load_up(0, (it - NB + 4) // 2, it % 2)

            def load_up(p, e, part):
                if e == 1:
                    sp.dma_start(up_sb[:, 1, part, :, :].bitcast(F32),
                                 up_t[p, :, 1, part, :, :]).then_inc(up_loaded, 16)
                    return
                for hs in range(HS):
                    load_up_slice(p, hs, part)

            def load_up_slice(p, hs, part):
                sp.dma_start(up_sb[:, 0, part, :, hs * 512:(hs + 1) * 512].bitcast(F32),
                             up_t[p, :, 0, part, :, hs * 512:(hs + 1) * 512]).then_inc(up_slice_loaded[hs], 16)

            def store_weights(it, w):
                if w == 0:
                    def dst(part):
                        return up_t[it // 16, :, (it // 8) % 2, part, :, bass.ds(it % 8 * P, P)]
                else:
                    def dst(part):
                        return down_t[(it % 4) // 2, :, it // 16, part, bass.ds((it % 2) * 4, 4),
                                      bass.ds((it // 4) % 4 * P, P)]
                sp.wait_ge(w_split[w], it + 1)
                settled(sp)
                sp.dma_start(dst(HI), w_hi[w][:, :, :].bitcast(F32)).then_inc(w_stored[w], 16)
                sp.dma_start(dst(LO), w_lo[w][:, :, :].bitcast(F32)).then_inc(w_stored[w], 16)
                if has(it + 1):
                    block_of = (wfc_block, wpr_block)[w]
                    sp.dma_start(wst[w][:, :], block_of(it + 1)).then_inc(wst_loaded[w], 16)

            iterations(sp, step)

            def load_down(p, e):
                slot = e if p == 0 else 2 - e
                for part in (HI, LO):
                    sp.dma_start(down_sb[:, slot, part, :, :].bitcast(F32),
                                 down_t[p, :, e, part, :, :]).then_inc(down_loaded[slot], 16)

            sp.wait_ge(scalar_left, 1)
            sp.wait_ge(vector_left, 1)
            sp.wait_ge(scattered, 16 * NB)
            sp.wait_ge(padded, 16)

            def load_rows(n):
                if not isinstance(n, int) or n >= 3:
                    sp.wait_ge(y_done, n - 2)
                    settled(sp)
                wait(sp, rows_loaded, 16 * n)
                if not isinstance(n, int):
                    settled(sp)
                sp.dma_start(rows_in[:, n % 3, :],
                             sorted_rows[bass.ds(n % NT * P, P), :]).then_inc(rows_loaded, 16)

            def store_part(n):
                sp.wait_ge(y_done, n + 1)
                settled(sp)
                sp.dma_start(partial[bass.ds(n * P, P), :], y_out[:, :]).then_inc(part_stored, 16)

            def load_part(n):
                wait(sp, part_loaded, 16 * (n - NT))
                if not isinstance(n, int):
                    settled(sp)
                sp.dma_start(part_in[:, n % 3, :],
                             partial[bass.ds((n - NT) * P, P), :]).then_inc(part_loaded, 16)

            for n in range(3):
                load_rows(n)
            sp.wait_ge(w_stored[1], 32 * NB)
            load_down(0, 0)
            load_down(0, 1)
            load_rows(3)
            store_part(0)
            load_down(1, 0)
            with sp.Fori(4, NT + 1) as n:
                load_rows(n)
                store_part(n - 3)
            sp.wait_ge(h_done, HS * (NT - 1) + 1)
            for part in (HI, LO):
                load_up_slice(1, 0, part)
            load_rows(NT + 1)
            store_part(NT - 2)
            sp.wait_ge(h_done, HS * NT)
            for part in (HI, LO):
                load_up_slice(1, 1, part)
            store_part(NT - 1)
            sp.wait_ge(part_stored, 16 * NT)
            load_part(NT)
            load_part(NT + 1)
            load_rows(NT + 2)
            load_part(NT + 2)
            for part in (HI, LO):
                load_up(1, 1, part)
            load_rows(NT + 3)
            load_part(NT + 3)
            sp.wait_ge(y_psum, HS * NT)
            load_down(1, 1)
            with sp.Fori(NT + 4, 2 * NT) as n:
                load_rows(n)
                load_part(n)

        @block.gpsimd
        def _(pool):
            pool.memset(ident[:, :], 0.0).then_inc(const_a, 1)
            pool.memset(upper[:, :], 1.0).then_inc(const_a, 1)
            pool.memset(ones[:, :], 1.0).then_inc(const_ready, 1)
            pool.memset(neghalf[:, :], -0.5).then_inc(const_ready, 1)
            pool.wait_ge(const_a, 2)
            pool.affine_select(out=ident[:, :], in_=ident[:, :], compare_op=ALU.not_equal, fill=1.0, base=0,
                               pattern=[[-1, P]], channel_multiplier=1).then_inc(const_ready, 1)
            pool.affine_select(out=upper[:, :], in_=upper[:, :], compare_op=ALU.is_gt, fill=0.0, base=0,
                               pattern=[[1, P]], channel_multiplier=-1).then_inc(const_ready, 1)
            pool.iota(ident_i[:, :], pattern=[[0, 1]], base=0, channel_multiplier=1).then_inc(const_ready, 1)
            pool.iota(starts_i[:, :], pattern=[[P, NT]], base=0, channel_multiplier=0).then_inc(const_ready, 1)
            pool.wait_ge(const_ready, 6)

            def power(dst, var, tmp, have, mid, done, b):
                pool.wait_ge(have, b + 1)
                settled(pool)
                pool.tensor_scalar(tmp[:, :], var, EPS, None, ALU.add).then_inc(mid, 1)
                pool.wait_ge(mid, b + 1)
                pool.tensor_tensor(dst, tmp[:, :], neghalf[:, :], ALU.pow).then_inc(done, 1)

            def values(it, b, g):
                wait(pool, pv_done, NQ * (b - 1) + NCH * (g + 1))
                pool.wait_ge(a_read, a_through(it - 1, 5, MORE))
                pool.tensor_copy(vt[:, g * GH:(g + 1) * GH, :, 0:DH],
                                 vt_next[:, b % RING, g * GH:(g + 1) * GH, :, :]).then_inc(v_half[g], 1)

            def split_weights(it, w):
                pool.wait_ge(w_rounded[w], it + 1)
                wait(pool, w_stored[w], 32 * it)
                pool.tensor_tensor(w_lo[w][:, :, :], w_raw[w][:, :, :], w_hi[w][:, :, :].bitcast(F32),
                                   ALU.subtract).then_inc(w_split[w], 1)

            def place(it, b):
                pool.wait_ge(a_read, a_through(it, 6, MORE))
                wait(pool, scattered, 16 * b)
                settled(pool)
                pool.tensor_tensor(ahead[:, :], ranks[:, 0:1], count1[:, :], ALU.add).then_inc(front_done, 1)
                pool.tensor_scalar(back[:, :], token[:, :], -float(CAP - 1), None, ALU.add).then_inc(back_done, 1)
                pool.wait_ge(front_done, 2 * b + 1)
                settled(pool)
                pool.tensor_tensor(front[:, :], token[:, :], ahead[:, :], ALU.subtract).then_inc(front_done, 1)
                pool.wait_ge(back_done, 3 * b + 1)
                settled(pool)
                pool.tensor_tensor(to_back[:, :], back[:, :], to_one[:, :], ALU.mult).then_inc(back_done, 1)
                pool.tensor_copy(row[:, M + 3:M + 4].bitcast(I32), token[:, :]).then_inc(row_done, 1)
                pool.tensor_tensor(row[:, M + 2:M + 3], row[:, M + 2:M + 3], row[:, M + 1:M + 2],
                                   ALU.mult).then_inc(row_done, 1)
                pool.wait_ge(front_done, 2 * b + 2)
                pool.wait_ge(back_done, 3 * b + 2)
                settled(pool)
                pool.tensor_tensor(slot_f[:, :], front[:, :], to_back[:, :], ALU.subtract).then_inc(back_done, 1)
                pool.wait_ge(back_done, 3 * b + 3)
                settled(pool)
                pool.tensor_copy(slot[:, :], slot_f[:, :]).then_inc(slot_done, 1)
                pool.tensor_scalar(token[:, :], token[:, :], float(P), None, ALU.add).then_inc(token_done, 1)
                pool.tensor_tensor(count1[:, :], count1[:, :], ranks[:, 1:2], ALU.add).then_inc(count_done, 1)

            def step(it):
                b = it + 3
                if has(it):
                    values(it, it, 1)
                if has(b):
                    pool.wait_ge(k1_done, b + 1)
                    wait(pool, k2_done, b)
                    pool.tensor_tensor(krest[:, :], c_in[:, :], kparts[:, 0, :], ALU.subtract).then_inc(krest_done, 1)
                    power(rstd1[:, :], mv1[:, 1:2], ve1, mv1_done, ve1_done, rstd1_done, b)
                if has(it - 1):
                    power(row[:, M + 1:M + 2], row[:, M + 1:M + 2], ve2, mv2_done, ve2_done, rstd2_done, it - 1)
                if has(it):
                    split_weights(it, 0)
                if has(b):
                    pool.wait_ge(k2_done, b + 1)
                    pool.wait_ge(krest_done, b + 1)
                    pool.tensor_tensor(kparts[:, 2, :], krest[:, :], kparts[:, 1, :], ALU.subtract).then_inc(k3_done, 1)
                if has(it + 1):
                    pool.wait_ge(v_read, v_through(it, 4, MORE))
                    wait(pool, c_stacked, 32 * (it + 1))
                    settled(pool)
                    pool.tensor_copy(cparts[:, 1, :], crest[:, :]).then_inc(c2_done, 1)
                    values(it, it + 1, 0)
                if has(it):
                    split_weights(it, 1)
                if has(b):
                    pool.wait_ge(q1_done, b + 1)
                    wait(pool, q2_done, b)
                    pool.tensor_tensor(qrest[:, :], qf[:, :], qparts[:, 0, :], ALU.subtract).then_inc(qrest_done, 1)
                    pool.wait_ge(q2_done, b + 1)
                    pool.wait_ge(qrest_done, b + 1)
                    pool.tensor_tensor(qparts[:, 2, :], qrest[:, :], qparts[:, 1, :], ALU.subtract).then_inc(q3_done, 1)
                if has(it - 1):
                    place(it, it - 1)
                    pool.wait_ge(slot_done, it)
                    pool.wait_ge(row_done, 2 * it)
                    settled(pool)
                    pool.indirect_dma_start(
                        out=sorted_rows[:, :], out_offset=bass.IndirectOffsetOnAxis(ap=slot[:, 0:1], axis=0),
                        in_=row[:, :], in_offset=None).then_inc(scattered, 16)

            iterations(pool, step)
            pool.wait_ge(pad_done, 1)
            pool.indirect_dma_start(
                out=sorted_rows[:, :], out_offset=bass.IndirectOffsetOnAxis(ap=pad_slot[:, 0:1], axis=0),
                in_=pad_row[:, :], in_offset=None).then_inc(padded, 16)

            with pool.Fori(NT, 2 * NT) as n:
                pool.wait_ge(y_done, n + 1)
                settled(pool)
                pool.indirect_dma_start(
                    out=out[:, :], out_offset=bass.IndirectOffsetOnAxis(ap=y_token[:, 0:1], axis=0),
                    in_=y_out[:, :], in_offset=None, bounds_check=NTOK - 1, oob_is_err=False).then_inc(y_stored, 16)
            pool.wait_ge(y_stored, 16 * NT)

        @block.scalar
        def _(sc):
            def exps(it, s):
                b, q = quad(it, s)
                if not has(b):
                    return
                for hh in range(GH):
                    sc.wait_ge(a_filled, a_through(it, s, hh))
                    if hh == 0:
                        wait(sc, pv_done, b * NQ + q - 3)
                    nc.scalar.activation(probs[:, q % 4, hh, :], a_slot(it, s, hh)[0][:, :], ACT.Exp,
                                         scale=SCALE).then_inc(a_read, 1)

            def step(it):
                b = it + 3
                for s in range(NQ):
                    if s == 0 and has(it - 1):
                        o_evac(it - 1, 1)
                    if s == 4 and has(it):
                        o_evac(it, 0)
                    exps(it, s)
                    if (s == 1 or s == 3) and has(it):
                        take_weights(it, s)
                    if s == 5 and has(b):
                        sc.wait_ge(a_filled, a_through(it, s, MORE))
                        wait(sc, v_half[1], b - RING + 1)
                        nc.scalar.activation(
                            vt_next[:, b % RING, :, :, :].rearrange("p h c d -> p c h d"),
                            a_slot(it, s, MORE)[0][:, :].rearrange("p (c d h) -> p c h d", c=NCH, h=H),
                            ACT.Copy).then_inc(a_read, 1)
                    if s == 6 and has(it - 1):
                        sc.wait_ge(a_filled, a_through(it, s, MORE))
                        wait(sc, count_done, it - 1)
                        nc.scalar.activation(ranks[:, :], a_slot(it, s, MORE)[0][:, 0:2],
                                             ACT.Copy).then_inc(a_read, 1)
                    if s == 2 and has(b):
                        sc.wait_ge(c_loaded, 16 * (b + 1))
                        wait(sc, k_stacked, 16 * SPLIT * b)
                        nc.scalar.activation(kparts[:, 0, :], c_in[:, :], ACT.Copy).then_inc(k1_done, 1)
                    if (s == 2 or s == 4) and has(it):
                        round_weights(it, s - 1)
                    if s == 4 and has(b):
                        sc.wait_ge(krest_done, b + 1)
                        nc.scalar.activation(kparts[:, 1, :], krest[:, :], ACT.Copy).then_inc(k2_done, 1)
                    if s == 6 and has(b):
                        sc.wait_ge(q_done, b + 1)
                        wait(sc, q_stacked, 16 * SPLIT * b)
                        nc.scalar.activation(qparts[:, 0, :], qf[:, :], ACT.Copy).then_inc(q1_done, 1)
                    if s == 7 and has(b):
                        sc.wait_ge(qrest_done, b + 1)
                        nc.scalar.activation(qparts[:, 1, :], qrest[:, :], ACT.Copy).then_inc(q2_done, 1)

            def take_weights(it, s):
                w = s // 2
                sc.wait_ge(a_filled, a_through(it, s, MORE))
                wait(sc, w_split[w], it)
                nc.scalar.activation(w_raw[w][:, :, :],
                                     a_slot(it, s, MORE)[0][:, :].rearrange("p (k n) -> p k n", k=NCH),
                                     ACT.Copy).then_inc(a_read, 1)

            def round_weights(it, s):
                w = s // 2
                sc.wait_ge(a_read, a_through(it, s, MORE))
                wait(sc, w_stored[w], 32 * it)
                nc.scalar.activation(w_hi[w][:, :, :], w_raw[w][:, :, :], ACT.Copy).then_inc(w_rounded[w], 1)

            def o_evac(b, g):
                sc.wait_ge(pv_done, NQ * b + NCH * (g + 1))
                if not isinstance(b, int) or b > 0:
                    sc.wait_ge(v_filled, v_through(b, 0, MORE) if g else v_through(b - 1, 6, MORE))
                nc.scalar.activation(o_sb[:, g, :], o_bank[:, :], ACT.Copy).then_inc(o_moved[g], 1)

            iterations(sc, step)
            nc.scalar.activation(left_mark[:, :], neghalf[:, :], ACT.Copy).then_inc(scalar_left, 1)
            sc.wait_ge(vector_left, 1)

            def round_rows(n):
                sc.wait_ge(f_t, n + 1)
                wait(sc, h_done, HS * n)
                nc.scalar.activation(f_lnt[:, HI, :, :], xt_bank[:, :].rearrange("p (k n) -> p k n", k=KC),
                                     ACT.Copy).then_inc(f_hi_done, 1)

            def tile(n, more=True):
                sc.wait_ge(absd_done, n + 1)
                wait(sc, den_done, n)
                nc.scalar.activation(expd[:, :], absd[:, :], ACT.Exp, scale=-1.0).then_inc(expd_done, 1)

                def turned(hs):
                    m = n * HS + hs
                    sc.wait_ge(a_t, m + 1)
                    wait(sc, y_psum, m - 1)
                    nc.scalar.activation(act_t[:, HI, 4 * hs:4 * hs + 4, :],
                                         at_bank[hs % 2][:, :].rearrange("p (k n) -> p k n", k=4),
                                         ACT.Copy).then_inc(a_hi_done, 1)

                def slice_(hs):
                    m = n * HS + hs
                    sc.wait_ge(h_done, m + 1)
                    nc.scalar.activation(half_h[:, hs % 2, :], h_bank[hs % 2][:, :], ACT.Copy,
                                         scale=0.5).then_inc(half_done, 1)
                    if hs == HS - 1 and more:
                        round_rows(n + 1)
                    sc.wait_ge(leaky_done, m + 1)
                    wait(sc, a_t, m - 1)
                    nc.scalar.activation(act[:, hs % 2, :], leaky[:, hs % 2, :], ACT.Square).then_inc(act_done, 1)

                slice_(0)
                turned(0)
                slice_(1)
                turned(1)

            round_rows(0)
            tile(0)
            with sc.Fori(1, 2 * NT - 1) as n:
                tile(n)
            tile(2 * NT - 1, more=False)

        @block.tensor
        def _(pe):
            pe.wait_ge(const_ready, 6)

            def transposed(src, dst, done):
                for k in range(NCH):
                    last = nc.tensor.transpose(dst[:, k * P:(k + 1) * P], src[:, k * P:(k + 1) * P], ident[:, :])
                last.then_inc(done, 1)

            def score(it, s, j):
                b, h = score_head(it, s)
                if h == 0 and j == 0:
                    pe.wait_ge(k_stacked, 16 * SPLIT * (b + 1))
                    pe.wait_ge(q_stacked, 16 * SPLIT * (b + 1))
                bank, before = v_slot(it, s, j)
                wait(pe, v_read, before)
                nc.tensor.matmul(bank[:, :], qst[0:KR, b % RING, h, j * P:(j + 1) * P],
                                 kst[0:KR, b % RING, h, :], start=True, stop=True).then_inc(v_filled, 1)

            def shift(it, s, hh):
                b, q = quad(it, s)
                h, c = (q // NCH) * GH + hh, q % NCH
                if q == 0 and hh == 0:
                    pe.wait_ge(c_stacked, 32 * (b + 1))
                    if isinstance(b, int) and b == 0:
                        pe.wait_ge(v_const, 2)
                bank, before = a_slot(it, s, hh)
                wait(pe, a_read, before)
                nc.tensor.matmul(bank[:, :], kst[0:KR + 2, b % RING, h, c * P:(c + 1) * P],
                                 qst[0:KR + 2, b % RING, h, :], start=True, stop=True).then_inc(a_filled, 1)

            def product(b, q):
                g, c = q // NCH, q % NCH
                pe.wait_ge(a_read, a_through(b, q - 1, GH - 1) if q else a_through(b - 1, NQ - 1, GH - 1))
                if c == 0:
                    pe.wait_ge(v_half[g], b + 1)
                    if g == 0:
                        wait(pe, o_moved[1], b)
                    else:
                        pe.wait_ge(o_moved[0], b + 1)
                for hh in range(GH):
                    last = nc.tensor.matmul(o_bank[32 * hh:32 * hh + 32, :], vt[:, g * GH + hh, c, :],
                                            probs[:, q % 4, hh, :], start=(c == 0), stop=(c == NCH - 1))
                last.then_inc(pv_done, 1)

            def more_for_scalar(it, s):
                if (s, MORE) not in A_ORDER or not a_exists(it, s, MORE):
                    return
                bank, before = a_slot(it, s, MORE)
                if s == 1 or s == 3:
                    pe.wait_ge(wst_loaded[s // 2], 16 * (it + 1))
                    wait(pe, a_read, before)
                    transposed(wst[s // 2], bank, a_filled)
                if s == 5:
                    pe.wait_ge(c_loaded, 16 * (it + 4))
                    wait(pe, a_read, before)
                    transposed(c_in, bank, a_filled)
                if s == 6:
                    pe.wait_ge(one_done, it)
                    wait(pe, a_read, before)
                    nc.tensor.matmul(bank[:, 0:1], upper[:, :], to_one[:, :], start=True, stop=True)
                    nc.tensor.matmul(bank[:, 1:2], ones[:, :], to_one[:, :], start=True,
                                     stop=True).then_inc(a_filled, 1)

            def more_for_vector(it, s):
                if (s, MORE) not in V_ORDER or not v_exists(it, s, MORE):
                    return
                bank, before = v_slot(it, s, MORE)
                wait(pe, v_read, before)
                if s == 0:
                    pe.wait_ge(o_moved[1], it)
                    transposed(o_sb[:, 1, :], bank, v_filled)
                if s == 2:
                    pe.wait_ge(v_read, v_through(it, 0, MORE))
                    for k in range(NCH):
                        last = nc.tensor.transpose(bank[:, k * P:(k + 1) * P], o_norm[:, k, :], ident[:, :])
                    last.then_inc(v_filled, 1)
                if s == 4:
                    pe.wait_ge(v_read, v_through(it, 3, NCH - 1))
                    pe.wait_ge(head_copied, it + 2)
                    nc.tensor.transpose(bank[0:H * NCH, 0:P], maxes[:, :], ident[:, :]).then_inc(v_filled, 1)
                if s == 6:
                    pe.wait_ge(o_moved[0], it + 1)
                    transposed(o_sb[:, 0, :], bank, v_filled)

            def step(it):
                for s in range(NQ):
                    for j in range(NCH):
                        if a_exists(it, s, j):
                            shift(it, s, j)
                        if v_exists(it, s, j):
                            score(it, s, j)
                    more_for_scalar(it, s)
                    if has(it):
                        product(it, s)
                    more_for_vector(it, s)

            iterations(pe, step)

            pe.wait_ge(scalar_left, 1)
            pe.wait_ge(vector_left, 1)
            pe.wait_ge(table_done, 1)

            def flip(n):
                pe.wait_ge(f_ln_done, n + 1)
                wait(pe, f_t_moved, n)
                transposed(f_ln, xt_bank, f_t)

            PRODUCTS = ((HI, HI), (LO, HI), (HI, LO))
            STEPS = 6
            assert (NT - 3) % STEPS == 0

            def tile(n, p, expert, before=None, ahead=True, more=True):
                def up(hs):
                    m = n * HS + hs
                    wait(pe, leaky_done, m - 1)
                    if first:
                        pe.wait_ge(up_slice_loaded[hs], 32 * (p + 1))
                    for k in range(KC):
                        for a, w in PRODUCTS:
                            last = nc.tensor.matmul(h_bank[hs % 2][:, :], f_lnt[:, a, k, :],
                                                    up_sb[:, expert, w, k, hs * 512:(hs + 1) * 512],
                                                    start=(k == 0 and (a, w) == PRODUCTS[0]),
                                                    stop=(k == KC - 1 and (a, w) == PRODUCTS[-1]))
                    last.then_inc(h_done, 1)

                first = isinstance(n, int) and n % NT == 0
                pe.wait_ge(f_t_moved, n + 1)
                pe.wait_ge(up_loaded, expert * 32 + (32 * p + 1))
                up(0)
                if not first:
                    if before is None:
                        before = expert_of_tile(n - 1)
                    down(n - 1, p, before, range(0, HC // 2))
                turn(n, 0)
                up(1)
                after = expert_of_tile(n + 1) if ahead else None
                if more:
                    flip(n + 1)
                if not first:
                    down(n - 1, p, before, range(HC // 2, HC - 1))
                turn(n, 1)
                if not first:
                    down(n - 1, p, before, range(HC - 1, HC))
                return expert, after

            def expert_of_tile(n):
                return pe.value_load(expert_of[0:1, bass.ds((n + NT) % NT, 1)], min_val=0, max_val=NE - 1)

            def turn(n, hs):
                m = n * HS + hs
                pe.wait_ge(act_done, m + 1)
                wait(pe, a_t_moved, m - 1)
                transposed(act[:, hs % 2, :], at_bank[hs % 2], a_t)

            def down(n, p, expert, chunks):
                if chunks[0] == 0:
                    if isinstance(n, int) and n % NT == 0:
                        pe.wait_ge(down_loaded[2 * p], 32)
                    pe.wait_ge(down_loaded[1], expert * 32 + (32 * p + 1))
                    wait(pe, y_done, n)
                place = expert if p == 0 else expert * -1 + 2
                for k in chunks:
                    if k % (HC // HS) == 0:
                        pe.wait_ge(a_t_moved, n * HS + k // (HC // HS) + 1)
                    for a, w in PRODUCTS:
                        last = nc.tensor.matmul(y_bank[:, :], act_t[:, a, k, :], down_sb[:, place, w, k, :],
                                                start=(k == 0 and (a, w) == PRODUCTS[0]),
                                                stop=(k == HC - 1 and (a, w) == PRODUCTS[-1]))
                    if (k + 1) % (HC // HS) == 0:
                        last.then_inc(y_psum, 1)

            flip(0)
            for p in range(2):
                end = (p + 1) * NT
                before, expert = tile(p * NT, p, expert_of_tile(p * NT))
                tile(p * NT + 1, p, expert, before, ahead=False)
                with pe.Fori(p * NT + 2, end - STEPS, STEPS) as n:
                    before, expert = None, expert_of_tile(n)
                    for k in range(STEPS):
                        before, expert = tile(n + k, p, expert, before, ahead=(k < STEPS - 1))
                before, expert = tile(end - 1, p, expert_of_tile(end - 1), ahead=False, more=(p == 0))
                down(end - 1, p, before, range(0, HC // 2))
                down(end - 1, p, before, range(HC // 2, HC))

        @block.vector
        def _(dve):
            nc.vector.memset(vt[:, :, :, DH:2 * DH], 1.0).then_inc(v_const, 1)
            nc.vector.memset(count1[:, :], 0.0).then_inc(count_init, 1)
            nc.vector.memset(pad_row[:, :], 0.0).then_inc(pad_a, 1)
            dve.wait_ge(const_ready, 6)
            nc.vector.tensor_copy(token[:, :], ident_i[:, :]).then_inc(count_init, 1)
            nc.vector.tensor_copy(starts[:, :], starts_i[:, :]).then_inc(table_a, 1)
            dve.wait_ge(wr_loaded, 32)
            nc.vector.tensor_tensor(wdiff[:, :], wdiff[:, :], weighted[:, :], ALU.subtract).then_inc(wdiff_ready, 1)
            dve.wait_ge(count_init, 2)
            dve.wait_ge(wdiff_ready, 1)

            def norm(it, s, b, g):
                dve.wait_ge(v_filled, v_through(it, s, MORE))
                got = v_slot(it, s, MORE)[0][:, :].rearrange("p (j h r) -> p j h r", j=NCH, h=GH)
                nc.vector.reciprocal(rsum[:, :, :], got[:, :, :, DH]).then_inc(rsum_done[g], 1)
                dve.wait_ge(rsum_done[g], b + 1)
                nc.vector.tensor_tensor(
                    o_norm[:, :, g * GH * DH:(g + 1) * GH * DH].rearrange("p j (h r) -> p j h r", h=GH),
                    got[:, :, :, 0:DH], rsum[:, :, :].unsqueeze(3).to_broadcast([P, NCH, GH, DH]),
                    ALU.mult).then_inc(v_read, 1)

            def maximum(it, s, j):
                _, h = score_head(it, s)
                dst = max_head if h < LEAD else maxes
                dve.wait_ge(v_filled, v_through(it, s, j))
                nc.vector.reduce_max(dst[:, h * NCH + j:h * NCH + j + 1], v_slot(it, s, j)[0][:, :],
                                     AX.X).then_inc(v_read, 1)

            def input_stats(b):
                if has(b):
                    dve.wait_ge(x_loaded, 16 * (b + 1))
                    nc.vector.bn_stats(stats1[:, :], x_in[:, :]).then_inc(stats1_done, 1)

            def queries(b):
                if has(b):
                    dve.wait_ge(rstd1_done, b + 1)
                    wait(dve, q1_done, b)
                    wait(dve, qrest_done, b)
                    nc.vector.tensor_scalar(qf[:, :], x_in[:, :], mv1[:, 0:1], rstd1[:, 0:1], ALU.subtract,
                                            ALU.mult).then_inc(q_done, 1)

            def step(it):
                b, r = it + 3, it - 1
                for s in range(NQ):
                    for j in range(NCH):
                        if (s, j) == (0, 0) and has(it + 1):
                            dve.wait_ge(v_read, v_through(it - 1, 7, NCH - 1))
                            nc.vector.tensor_copy(maxes[:, 0:LEAD * NCH], max_head[:, :]).then_inc(head_copied, 1)
                        if (s, j) == (1, 1):
                            input_stats(b)
                        if (s, j) == (5, 2):
                            queries(b)
                            if isinstance(it, int) and it == -3:
                                nc.vector.memset(kst[KR:KR + 2, :, :, :], 1.0).then_inc(v_const, 1)
                        if (s, j) == (1, 2) and has(b):
                            dve.wait_ge(stats1_done, b + 1)
                            wait(dve, ve1_done, b)
                            settled(dve)
                            nc.vector.bn_aggr(mv1[:, :], stats1[:, :]).then_inc(mv1_done, 1)
                        if (s, j) == (3, 1) and has(r):
                            dve.wait_ge(v_read, v_through(it, 2, MORE))
                            nc.vector.bn_stats(stats2[:, :], row[:, 0:M]).then_inc(stats2_done, 1)
                        if (s, j) == (3, 2) and has(r):
                            dve.wait_ge(stats2_done, r + 1)
                            settled(dve)
                            nc.vector.bn_aggr(row[:, M:M + 2], stats2[:, :]).then_inc(mv2_done, 1)
                        if (s, j) == (3, 3) and has(r):
                            dve.wait_ge(mv2_done, r + 1)
                            nc.vector.scalar_tensor_tensor(
                                out=weighted[:, :], in0=row[:, 0:M], scalar=row[:, M:M + 1], in1=wdiff[:, :],
                                op0=ALU.subtract, op1=ALU.mult, accum_out=row[:, M + 2:M + 3]).then_inc(ldiff_done, 1)
                        if (s, j) == (4, 1) and has(r):
                            dve.wait_ge(ldiff_done, r + 1)
                            wait(dve, slot_done, r)
                            nc.vector.tensor_scalar(to_one[:, :], row[:, M + 2:M + 3], 0.0, None,
                                                    ALU.is_gt).then_inc(one_done, 1)
                        if (s, j) == (4, 0) and has(it + 1):
                            dve.wait_ge(head_copied, it + 2)
                        if v_exists(it, s, j):
                            maximum(it, s, j)
                    if s == 0 and has(r):
                        norm(it, s, r, 1)
                    if s == 2 and has(r):
                        dve.wait_ge(v_filled, v_through(it, 2, MORE))
                        dve.wait_ge(res_loaded, 16 * (r + 1))
                        wait(dve, scattered, 16 * r)
                        nc.vector.tensor_tensor(row[:, 0:M], v_slot(it, 2, MORE)[0][:, :], x_res[:, :],
                                                ALU.add).then_inc(v_read, 1)
                    if s == 4 and has(it + 1):
                        shifts(it, it + 1)
                    if s == 6 and has(it):
                        norm(it, s, it, 0)

            def shifts(it, b):
                dve.wait_ge(v_filled, v_through(it, 4, MORE))
                wait(dve, c_stacked, 32 * b)
                top = v_slot(it, 4, MORE)[0][0:H * NCH, 0:P]
                nc.vector.tensor_scalar(cparts[:, 0, :], top, -1.0, None, ALU.mult).then_inc(c1_done, 1)
                dve.wait_ge(c1_done, b + 1)
                nc.vector.scalar_tensor_tensor(out=crest[:, :], in0=top, scalar=-1.0, in1=cparts[:, 0, :],
                                               op0=ALU.mult, op1=ALU.subtract).then_inc(v_read, 1)

            iterations(dve, step)

            dve.wait_ge(pad_a, 1)
            dve.wait_ge(count_done, NB)
            nc.vector.memset(pad_row[:, M + 3:M + 4].bitcast(I32), NTOK).then_inc(pad_a, 1)
            nc.vector.tensor_scalar(pad_f[:, :], count1[:, :], -1.0, float(NTOK), ALU.mult, ALU.add).then_inc(pad_a, 1)
            dve.wait_ge(pad_a, 3)
            nc.vector.tensor_tensor(pad_slot[:, :], pad_f[:, :], ident_i[:, :], ALU.add).then_inc(pad_done, 1)
            dve.wait_ge(table_a, 1)
            nc.vector.tensor_scalar(expert_of[:, :], starts[:, :], pad_f[0:1, 0:1], None, ALU.is_gt).then_inc(table_done, 1)
            dve.wait_ge(padded, 16)
            nc.vector.tensor_copy(left_mark2[:, :], neghalf[:, :]).then_inc(vector_left, 1)
            dve.wait_ge(scalar_left, 1)

            def normalise(i):
                dve.wait_ge(rows_loaded, 16 * (i + 1))
                wait(dve, f_t, i)
                nc.vector.tensor_scalar(f_ln[:, :], rows_in[:, i % 3, 0:M], rows_in[:, i % 3, M:M + 1],
                                        rows_in[:, i % 3, M + 1:M + 2], ALU.subtract,
                                        ALU.mult).then_inc(f_ln_done, 1)
                wait(dve, absd_done, i)
                nc.vector.tensor_scalar(negd[:, :], rows_in[:, i % 3, M + 2:M + 3], -1.0, None,
                                        ALU.mult).then_inc(negd_done, 1)
                dve.wait_ge(negd_done, i + 1)
                wait(dve, expd_done, i)
                nc.vector.tensor_tensor(absd[:, :], rows_in[:, i % 3, M + 2:M + 3], negd[:, :],
                                        ALU.max).then_inc(absd_done, 1)

            def take(i):
                dve.wait_ge(f_t, i + 1)
                dve.wait_ge(f_hi_done, i + 1)
                nc.vector.tensor_tensor(f_lnt[:, LO, :, :], xt_bank[:, :].rearrange("p (k n) -> p k n", k=KC),
                                        f_lnt[:, HI, :, :].bitcast(F32), ALU.subtract).then_inc(f_t_moved, 1)

            def leak(i, hs):
                n = i * HS + hs
                dve.wait_ge(half_done, n + 1)
                wait(dve, act_done, n - 1)
                nc.vector.tensor_tensor(leaky[:, hs % 2, :], h_bank[hs % 2][:, :], half_h[:, hs % 2, :],
                                        ALU.max).then_inc(leaky_done, 1)

            def turned(i, hs):
                dve.wait_ge(a_hi_done, i * HS + hs + 1)
                nc.vector.tensor_tensor(act_t[:, LO, 4 * hs:4 * hs + 4, :],
                                        at_bank[hs % 2][:, :].rearrange("p (k n) -> p k n", k=4),
                                        act_t[:, HI, 4 * hs:4 * hs + 4, :].bitcast(F32),
                                        ALU.subtract).then_inc(a_t_moved, 1)

            def weigh(i):
                dve.wait_ge(expd_done, i + 1)
                nc.vector.tensor_scalar(den[:, :], expd[:, :], 1.0, None, ALU.add).then_inc(den_done, 1)
                dve.wait_ge(den_done, i + 1)
                nc.vector.reciprocal(top_w[:, :], den[:, :]).then_inc(top_done, 1)

            def sum_up(i, second):
                dve.wait_ge(y_psum, (i + 1) * HS)
                dve.wait_ge(top_done, i + 1)
                if not second or (isinstance(i, int) and i == NT):
                    wait(dve, part_stored, 16 * i)
                else:
                    dve.wait_ge(y_stored, 16 * (i - NT))
                so_far = rows_in[:, i % 3, 0:M]
                if second:
                    dve.wait_ge(part_loaded, 16 * (i - NT + 1))
                    so_far = part_in[:, i % 3, :]
                nc.vector.scalar_tensor_tensor(out=y_out[:, :], in0=y_bank[:, :], scalar=top_w[:, 0:1],
                                               in1=so_far, op0=ALU.mult, op1=ALU.add).then_inc(y_summed, 1)
                nc.vector.tensor_copy(y_token[:, :], rows_in[:, i % 3, M + 3:M + 4].bitcast(I32)).then_inc(y_done, 1)

            def tile(i, second, more=True):
                leak(i, 0)
                if more:
                    normalise(i + 1)
                turned(i, 0)
                leak(i, 1)
                if more:
                    take(i + 1)
                if not isinstance(i, int) or i % NT:
                    sum_up(i - 1, second)
                weigh(i)
                turned(i, 1)

            normalise(0)
            take(0)
            for p in range(2):
                end = (p + 1) * NT
                tile(p * NT, p == 1)
                tile(p * NT + 1, p == 1)
                with dve.Fori(p * NT + 2, end - 1) as n:
                    tile(n, p == 1)
                tile(end - 1, p == 1, more=(p == 0))
                sum_up(end - 1, p == 1)


_INS = ["x", "ctx_2048", "L0_ffn_w_router", "L0_ffn_w_fc", "L0_ffn_w_proj"]


def kernel(**inputs):
    import concourse.bacc as bacc
    import numpy as np
    from concourse import mybir as _mybir
    from concourse.bass_utils import run_bass_kernel_spmd

    nc = bacc.Bacc("TRN2", target_bir_lowering=False, num_devices=1)
    arrays, args = {}, []
    for name in _INS:
        a = np.ascontiguousarray(inputs[name])
        arrays[f"in_{name}"] = a
        args.append(nc.dram_tensor(f"in_{name}", a.shape, _mybir.dt.from_np(a.dtype), kind="ExternalInput").ap())
    batches, rows, feats = inputs["x"].shape
    out = nc.dram_tensor("out", (batches * rows, feats), _mybir.dt.float32, kind="ExternalOutput").ap()
    build_program(nc, *args, out)
    r = run_bass_kernel_spmd(nc, [arrays], core_ids=[0])
    return r.results[0]["out"].reshape(batches, rows, feats)
```
